# Optimizing a Trainium2 kernel written in Bass

```python
import numpy as np
import jax
import jax.numpy as jnp

def _softmax(x, axis=-1):
    return jax.nn.softmax(x, axis=axis)

def _gelu(x):
    return jax.nn.gelu(x, approximate=True)

def _silu(x):
    return jax.nn.silu(x)

def _sigmoid(x):
    return jax.nn.sigmoid(x)

def _layernorm(x, axis=-1, eps=1e-05):
    m = jnp.mean(x, axis=axis, keepdims=True)
    v = jnp.var(x, axis=axis, keepdims=True)
    return (x - m) / jnp.sqrt(v + eps)

def _scatter_add(tgt, idx, src, axis=0):
    return tgt.at[idx].add(src)

def _segment_sum(src, seg, n):
    return jax.ops.segment_sum(src, seg, n)
kernel_name = 'mk_gnn_resnorm_d2_gnn_r64_d3580a'

def setup_inputs(seed: int=0):
    np.random.seed(seed)
    _w = jnp.asarray

    def _rec_inputs():
        import jax
        import jax.numpy as jnp
        _gk = jax.random.key(seed)
        x = -0.000202 + 1 * jax.random.normal(jax.random.fold_in(_gk, 1), (50000, 128), jnp.float32)
        src = jax.random.randint(jax.random.fold_in(_gk, 2), (25000,), 0, 50000, jnp.int32)
        dst = jax.random.randint(jax.random.fold_in(_gk, 3), (25000,), 0, 50000, jnp.int32)
        _o = jnp.argsort(dst, stable=True)
        src = src[_o]
        dst = dst[_o]
        edge_attr3_4x1 = jax.random.uniform(jax.random.fold_in(_gk, 12), (25000, 4, 1), jnp.float32, 0.0, 1)
        edge_attr_70 = 0.000111316 + 1.00009 * jax.random.normal(jax.random.fold_in(_gk, 13), (25000, 70), jnp.float32)
        return (x, src, dst, edge_attr3_4x1, edge_attr_70)
    x, src, dst, edge_attr3_4x1, edge_attr_70 = _rec_inputs()

    def _L0_gnn_setup():
        import jax, jax.numpy as jnp
        import numpy as np
        N_NODES = 50000
        IN_C = 128
        OUT_C = 128
        EDGE_F = 65
        N_EDGES = 12500
        EDGE_ATTR_COLS = 70
        key = jax.random.key(seed)
        ks = jax.random.split(key, 10)
        fcat = 3 * IN_C + EDGE_F
        sc = lambda d: 1.0 / np.sqrt(d)
        return {'x': jax.random.normal(ks[0], (N_NODES, IN_C), dtype=jnp.float32), 'edge_index': jax.random.randint(ks[1], (2, N_EDGES), 0, N_NODES, dtype=jnp.int32), 'edge_attr': jax.random.normal(ks[2], (N_EDGES, EDGE_ATTR_COLS), dtype=jnp.float32), 'Wf': jax.random.normal(ks[3], (fcat, IN_C), dtype=jnp.float32) * sc(fcat), 'bf': jnp.zeros((IN_C,), dtype=jnp.float32), 'Wq': jax.random.normal(ks[4], (IN_C, IN_C), dtype=jnp.float32) * sc(IN_C), 'Wk': jax.random.normal(ks[5], (IN_C, IN_C), dtype=jnp.float32) * sc(IN_C), 'Wa': jax.random.normal(ks[6], (IN_C, 1), dtype=jnp.float32) * sc(IN_C), 'Wu': jax.random.normal(ks[7], (IN_C, OUT_C), dtype=jnp.float32) * sc(IN_C), 'bu': jnp.zeros((OUT_C,), dtype=jnp.float32)}
    _L0_gnn_all = _L0_gnn_setup()
    _L0_gnn_in = {k: v for k, v in _L0_gnn_all.items() if k in ('Wf', 'bf', 'Wq', 'Wk', 'Wa', 'Wu', 'bu')}
    del _L0_gnn_all

    def _L1_gnn_setup():
        import jax, jax.numpy as jnp
        import numpy as np
        N_NODES = 50000
        N_EDGES = 12500
        N_HEADS = 4
        FEAT = 128
        key = jax.random.key(seed)
        k1, k2, k3, k4 = jax.random.split(key, 4)
        h = jax.random.normal(k1, (N_NODES, FEAT), dtype=jnp.float32)
        e = jax.random.uniform(k2, (N_EDGES, N_HEADS, 1), dtype=jnp.float32)
        src = jax.random.randint(k3, (N_EDGES,), 0, N_NODES, dtype=jnp.int64)
        dst = jax.random.randint(k4, (N_EDGES,), 0, N_NODES, dtype=jnp.int64)
        return {'h': h, 'e': e, 'src': src, 'dst': dst}
    _L1_gnn_all = _L1_gnn_setup()
    _L1_gnn_in = {k: v for k, v in _L1_gnn_all.items() if k in ()}
    del _L1_gnn_all
    return {'x': x, 'src': src, 'dst': dst, 'edge_attr3_4x1': edge_attr3_4x1, 'edge_attr_70': edge_attr_70, 'L0_gnn_Wf': _L0_gnn_in['Wf'], 'L0_gnn_bf': _L0_gnn_in['bf'], 'L0_gnn_Wq': _L0_gnn_in['Wq'], 'L0_gnn_Wk': _L0_gnn_in['Wk'], 'L0_gnn_Wa': _L0_gnn_in['Wa'], 'L0_gnn_Wu': _L0_gnn_in['Wu'], 'L0_gnn_bu': _L0_gnn_in['bu']}

def reference(x, src, dst, edge_attr3_4x1, edge_attr_70, L0_gnn_Wf, L0_gnn_bf, L0_gnn_Wq, L0_gnn_Wk, L0_gnn_Wa, L0_gnn_Wu, L0_gnn_bu):
    import jax
    import jax.numpy as jnp

    def _L0_gnn_ref(x, edge_index, edge_attr, Wf, bf, Wq, Wk, Wa, Wu, bu):
        import jax, jax.numpy as jnp
        import numpy as np
        N_NODES = 50000
        IN_C = 128
        OUT_C = 128
        EDGE_F = 65
        N_EDGES = 12500
        EDGE_ATTR_COLS = 70
        src = edge_index[0]
        tgt = edge_index[1]
        ni = x[src]
        nj = x[tgt]
        mask = (edge_attr[:, 0:1] < 8).astype(x.dtype)
        fcat = jnp.concatenate([ni, nj, ni - nj, edge_attr[:, :EDGE_F]], axis=1)
        f = jax.nn.elu(fcat @ Wf + bf) * mask
        scale = IN_C ** (-0.5)
        q = ni @ Wq
        k = f @ Wk
        a = jnp.tanh(q * k * scale @ Wa)
        numerator = jnp.exp(a)
        a_sum = jax.ops.segment_sum(a, src, num_segments=N_NODES)
        denominator = jnp.exp(a_sum)[src]
        s = numerator / denominator
        z = s * f
        aggr = jax.ops.segment_sum(z, src, num_segments=N_NODES)
        return (x + aggr) @ Wu + bu

    def _L1_gnn_ref(h, e, src, dst):
        import jax, jax.numpy as jnp
        import numpy as np
        N_NODES = 50000
        N_EDGES = 12500
        N_HEADS = 4
        FEAT = 128
        N = h.shape[0]
        H = e.shape[-2]
        x = h.reshape(N, H, -1)
        src2 = jnp.concatenate([src, dst])
        dst2 = jnp.concatenate([dst, src])
        e2 = jnp.concatenate([e, e], axis=0)
        e_sum = jax.ops.segment_sum(e2, dst2, num_segments=N)
        e2 = e2 / e_sum[dst2]
        gamma = 0.0
        loop = jnp.arange(N, dtype=src.dtype)
        src3 = jnp.concatenate([src2, loop])
        dst3 = jnp.concatenate([dst2, loop])
        e3 = jnp.concatenate([e2, jnp.full((N, H, 1), gamma, dtype=e.dtype)], axis=0)
        e3 = jnp.where((src3 == dst3)[:, None, None], gamma, e3)

        def f(y):
            return jax.ops.segment_sum(y[src3] * e3, dst3, num_segments=N)
        dt = jnp.asarray(1.0, dtype=h.dtype)
        k1 = f(x)
        k2 = f(x + dt * k1 / 3)
        k3 = f(x + dt * (k2 - k1 / 3))
        k4 = f(x + dt * (k1 - k2 + k3))
        y = x + dt * 0.125 * (k1 + 3 * (k2 + k3) + k4)
        return y.reshape(N, -1)
    edge_index = jnp.stack([src, dst])
    x = _layernorm(x + _L0_gnn_ref(x, edge_index, edge_attr_70, L0_gnn_Wf, L0_gnn_bf, L0_gnn_Wq, L0_gnn_Wk, L0_gnn_Wa, L0_gnn_Wu, L0_gnn_bu), axis=-1)
    x = _layernorm(x + _L1_gnn_ref(x, edge_attr3_4x1, src, dst), axis=-1)
    return x

_drawn_inputs = setup_inputs


def setup_inputs(seed=0):
    import zlib

    import numpy as np

    out = dict(_drawn_inputs(seed))
    spreads = {'L0_gnn_bf': (0.0, 0.1), 'L0_gnn_bu': (0.0, 0.1)}
    factors = {'L0_gnn_Wq': 3.77, 'L0_gnn_Wk': 3.805, 'L0_gnn_Wa': 3.708}
    for name, (base, spread) in spreads.items():
        noise = np.random.default_rng([zlib.crc32(name.encode()), seed]).standard_normal(out[name].shape)
        drawn = base * np.exp(spread * noise) if base else spread * noise
        out[name] = jnp.asarray(drawn.astype(out[name].dtype))
    for name, factor in factors.items():
        out[name] = (out[name] * factor).astype(out[name].dtype)
    return out
```

```python
from contextlib import ExitStack

import concourse.bass as bass
from concourse import mybir

F32 = mybir.dt.float32
I32 = mybir.dt.int32
ALU = mybir.AluOpType
ACT = mybir.ActivationFunctionType
AX = mybir.AxisListType

N = 50000
E = 25000
D = 128
H = 4
HF = D // H
EF = 65
EC = 70
Q = 4
ST = Q * 128
NS = -(-E // ST)
NT = NS * Q
NP = NT * 128
HALF = NT // 2
TAIL = E - (NT - 1) * 128
ROWS = 50688
AW = D + 4
UW = D + 8
KEY, W, EV, SC = Q, 2 * Q, 2 * Q + Q * H, 2 * Q + 2 * Q * H
META = SC + Q
R = 6
NCH = (N // 128) // R
NMAIN = NCH * R * 128
NREST = N - NMAIN
ZW = 44 * UW
EPS = 1e-5


def steps(eng, body, n, m=2, peel=1):
    for s in range(m * peel):
        body(s, s % m, s // m)
    with eng.Fori(peel, n // m) as k:
        for i in range(m):
            body(k * m + i, i, k)
    for s in range(n // m * m, n):
        body(s, s % m, s // m)


def back(slot, k, d, m):
    return (slot - d) % m, k - (1 if slot < d else 0)


def known(s):
    return isinstance(s, int)


def build(nc, x, src, dst, e_in, ea_in, Wf, bf, Wq, Wk, Wa, Wu, bu, out):
    key_rows = nc.dram_tensor("key_rows", (2 * NP,), I32).ap()
    meta_d = nc.dram_tensor("meta_d", (128, 2 * NS, META), F32).ap()
    agg = nc.dram_tensor("agg", (ROWS, AW), F32).ap()
    x1 = nc.dram_tensor("x1", (N, D), F32).ap()
    u = [nc.dram_tensor(f"u{i}", (ROWS, UW), F32).ap() for i in range(3)]

    with ExitStack() as ctx:
        def sb(name, shape, dt=F32):
            return ctx.enter_context(nc.sbuf_tensor(name, shape, dt))

        def sem(name):
            return ctx.enter_context(nc.semaphore(name))

        bank = [ctx.enter_context(nc.psum_tensor(f"bank{i}", [128, 512], F32)) for i in range(8)]

        ident = sb("ident", [128, 128])
        pos_i = sb("pos_i", [128, ST], I32)
        part_i = sb("part_i", [128, Q], I32)
        pos = sb("pos", [128, ST])
        part = sb("part", [128, Q])
        before = sb("before", [128, Q, ST])
        spare = sb("spare", [128, Q])
        zero = sb("zero", [128, ZW])
        ones = sb("ones", [1, 128])
        minus_half = sb("minus_half", [128, R])
        rows_i = sb("rows_i", [HALF, 2, 2, 128], I32)
        rows_f = sb("rows_f", [HALF, 4, 128])
        key = sb("key", [128, 2 * NT])
        e_sb = sb("e_sb", [128, NT, H])
        differ = sb("differ", [128, NT])
        earlier = sb("earlier", [128, 2 * NT])
        col_tmp = sb("col_tmp", [128, 2 * NS, Q])
        meta = sb("meta", [128, 2 * NS, META])
        meta_i = meta[:, :, :].bitcast(I32)
        key_row = [sb(f"key_row{i}", [128, ST], I32) for i in range(2)]
        same = [sb(f"same{i}", [128, Q, ST]) for i in range(2)]
        w_raw = sb("w_raw", [128, 3, D])
        w_attr = sb("w_attr", [EF + 1, D])
        w_src = sb("w_src", [128, 2, D])
        w_dst = sb("w_dst", [128, D])
        wqk = sb("wqk", [128, 2, D])
        wqk_t = sb("wqk_t", [128, 2, D])
        wa = sb("wa", [128, 1])
        wu = sb("wu", [128, D])
        bu_row = sb("bu_row", [1, D])
        src_row = [sb(f"src_row{i}", [128, Q], I32) for i in range(2)]
        early = [sb(f"early{i}", [128, SC]) for i in range(2)]
        sc_row = [sb(f"sc_row{i}", [128, Q]) for i in range(2)]
        xs = [sb(f"xs{i}", [128, Q, UW]) for i in range(2)]
        xd = [sb(f"xd{i}", [128, Q, D]) for i in range(2)]
        attr = [sb(f"attr{i}", [128, Q, EF + 1]) for i in range(2)]
        xs_t = sb("xs_t", [128, ST])
        xd_t = sb("xd_t", [128, ST])
        attr_t = sb("attr_t", [EF + 1, ST])
        neg = sb("neg", [128, ST])
        ex = sb("ex", [128, ST])
        act_f = sb("act_f", [128, ST])
        prod = sb("prod", [128, ST])
        mask = sb("mask", [128, Q])
        logit = sb("logit", [128, Q])
        att = sb("att", [128, Q])
        exp_att = sb("exp_att", [128, Q])
        z = [sb(f"z{i}", [128, Q, UW]) for i in range(2)]
        za = [sb(f"za{i}", [128, Q, AW]) for i in range(2)]
        summed = [sb(f"summed{i}", [128, Q, UW]) for i in range(2)]
        summed_a = [sb(f"summed_a{i}", [128, Q, AW]) for i in range(2)]
        inv = sb("inv", [128, Q, H])
        wn = sb("wn", [128, Q, H])
        xc = [sb(f"xc{i}", [128, R, D]) for i in range(4)]
        uc = [[sb(f"uc{j}_{i}", [128, R, UW]) for i in range(4)] for j in range(3)]
        agc = [uc[0][i][:, :, 0:AW] for i in range(4)]
        decay = sb("decay", [128, 4, R])
        xa = sb("xa", [128, R, D])
        xa_t = sb("xa_t", [128, R * 128])
        res = [sb(f"res{i}", [128, R, D]) for i in range(2)]
        stats = sb("stats", [128, R, 6])
        mv = [sb(f"mv{i}", [128, R, 2]) for i in range(2)]
        rstd = [sb(f"rstd{i}", [128, R]) for i in range(2)]
        normed = [sb(f"normed{i}", [128, R, D]) for i in range(2)]
        cinv = sb("cinv", [128, R, H])
        isolated = sb("isolated", [128, R])

        iota_done, pads_set, rows_in, e_in_sem, w_in, w_in2 = (sem(n) for n in (
            "iota_done", "pads_set", "rows_in", "e_in", "w_in", "w_in2"))
        const_done, zero_done, rows_f_done, key_t_done, key_done = (sem(n) for n in (
            "const_done", "zero_done", "rows_f_done", "key_t_done", "key_done"))
        key_rows_out, meta_out, agg_zeroed, u_zeroed, prep_v, w_t, w_tc, w_m, w_done, e_zero = (sem(n) for n in (
            "key_rows_out", "meta_out", "agg_zeroed", "u_zeroed", "prep_v", "w_t", "w_tc", "w_m", "w_done",
            "e_zero"))
        kr_in = [sem(f"p_kr_in{i}") for i in range(2)]
        kr_used = sem("p_kr_used")
        prep_c, prep_w, z_set = sem("prep_c"), sem("prep_w"), sem("z_set")
        sp_gate, pool_gate = sem("sp_gate"), sem("pool_gate")

        with nc.Block() as block:
            @block.gpsimd
            def _(g):
                g.iota(pos_i[:, :], [[1, ST]], base=0, channel_multiplier=0).then_inc(iota_done, 1)
                g.iota(part_i[:, :], [[128, Q]], base=0, channel_multiplier=1).then_inc(iota_done, 1)
                for d in range(2):
                    g.iota(rows_i[:, d, 1, :], [[1, 128]], base=N + (Q - 1) * 128,
                           channel_multiplier=0).then_inc(pads_set, 1)

            @block.sync
            def _(sp):
                sp.dma_start(w_raw[:, :, :], Wf[0:3 * D, :].rearrange("(k p) n -> p k n", p=128)).then_inc(w_in, 16)
                sp.dma_start(w_attr[0:EF, :], Wf[3 * D:3 * D + EF, :]).then_inc(w_in, 16)
                sp.dma_start(w_attr[EF:EF + 1, :], bf.rearrange("(o n) -> o n", o=1)).then_inc(w_in, 16)
                sp.dma_start(wqk[:, 0, :], Wq[:, :]).then_inc(w_in, 16)
                sp.dma_start(wqk[:, 1, :], Wk[:, :]).then_inc(w_in, 16)
                sp.dma_start(wa[:, :], Wa[:, :]).then_inc(w_in, 16)
                sp.dma_start(wu[:, :], Wu[:, :]).then_inc(w_in, 16)
                sp.dma_start(bu_row[:, :], bu.rearrange("(o n) -> o n", o=1)).then_inc(w_in, 16)
                sp.wait_ge(pads_set, 2)
                first = HALF * 128
                for d, ends in enumerate((src, dst)):
                    sp.dma_start(rows_i[:, d, 0, :], ends[0:first].rearrange("(r c) -> r c", c=128)
                                 ).then_inc(rows_in, 16)
                    sp.dma_start(rows_i[0:HALF - 1, d, 1, :],
                                 ends[first:first + (HALF - 1) * 128].rearrange("(r c) -> r c", c=128)
                                 ).then_inc(rows_in, 16)
                    sp.dma_start(rows_i[HALF - 1:HALF, d, 1, 0:TAIL],
                                 ends[E - TAIL:E].rearrange("(o n) -> o n", o=1)).then_inc(rows_in, 16)
                sp.wait_ge(rows_in, 96)
                for d in range(2):
                    for h in range(2):
                        sp.dma_start(key_rows[(2 * d + h) * first:(2 * d + h + 1) * first]
                                     .rearrange("(r c) -> r c", c=128), rows_i[:, d, h, :]).then_inc(key_rows_out, 16)
                sp.wait_ge(e_zero, 1)
                sp.dma_start(e_sb[:, 0:NT - 1, :], e_in[0:E - TAIL, :, 0].rearrange("(t p) h -> p t h", p=128)
                             ).then_inc(e_in_sem, 16)
                sp.dma_start(e_sb[0:TAIL, NT - 1, :], e_in[E - TAIL:E, :, 0]).then_inc(e_in_sem, 16)
                sp.wait_ge(key_rows_out, 64)

                def load_key_row(s, par, k):
                    if not (known(k) and k == 0):
                        sp.wait_ge(kr_used, s - 1)
                        sp.sem_inc(sp_gate, 1)
                    sp.dma_start(key_row[par][:, :], key_rows[bass.ds(s * ST, ST)]
                                 .rearrange("(o n) -> o n", o=1).to_broadcast([128, ST])).then_inc(kr_in[par], 16)
                steps(sp, load_key_row, 2 * NS)
                sp.wait_ge(prep_v, 1)
                sp.dma_start(meta_d[:, :, :], meta[:, :, :]).then_inc(meta_out, 16)
                sp.wait_ge(meta_out, 16)

            @block.scalar
            def _(act):
                act.wait_ge(zero_done, 1)
                for c in range(9):
                    act.dma_start(agg.rearrange("(p r) w -> p (r w)", p=128)[:, c * 44 * AW:(c + 1) * 44 * AW],
                                  zero[:, 0:44 * AW]).then_inc(agg_zeroed, 16)
                for i in range(3):
                    for c in range(9):
                        act.dma_start(u[i].rearrange("(p r) w -> p (r w)", p=128)[:, c * ZW:(c + 1) * ZW],
                                      zero[:, :]).then_inc(u_zeroed, 16)

            @block.tensor
            def _(pe):
                pe.wait_ge(rows_f_done, 1)
                pe.wait_ge(const_done, 3)
                for i in range(4):
                    t = pe.transpose(bank[0][:, i * HALF:(i + 1) * HALF], rows_f[:, i, :], ident[0:HALF, 0:HALF])
                t.then_inc(key_t_done, 1)
                pe.wait_ge(w_in, 128)
                pe.transpose(bank[1][:, 0:128], wqk[:, 0, :], ident[:, :])
                pe.transpose(bank[1][:, 128:256], wqk[:, 1, :], ident[:, :]).then_inc(w_t, 1)
                pe.wait_ge(w_tc, 2)
                pe.matmul(bank[2][:, 0:128], wqk_t[:, 0, :], wqk_t[:, 1, :], start=True, stop=True).then_inc(w_m, 1)

            @block.vector
            def _(v):
                v.memset(zero[:, :], 0.0).then_inc(zero_done, 1)
                v.memset(e_sb[:, NT - 1, :], 0.0).then_inc(e_zero, 1)
                v.memset(ones[:, :], 1.0).then_inc(const_done, 1)
                v.wait_ge(iota_done, 2)
                v.tensor_copy(pos[:, :], pos_i[:, :]).then_inc(prep_c, 1)
                v.tensor_copy(part[:, :], part_i[:, :]).then_inc(prep_c, 1)
                v.wait_ge(rows_in, 96)
                v.tensor_copy(rows_f[:, :, :], rows_i[:, :, :, :].rearrange("r d h c -> r (d h) c")
                              ).then_inc(rows_f_done, 1)
                v.wait_ge(prep_c, 2)
                v.tensor_scalar(ident[:, :], pos[:, 0:128], part[:, 0:1], None, ALU.is_equal).then_inc(const_done, 1)
                v.tensor_scalar(spare[:, :], part[:, :], float(N), None, ALU.add).then_inc(const_done, 1)
                for a in range(Q):
                    v.tensor_scalar(before[:, a, :], pos[:, :], part[:, a:a + 1], None, ALU.is_lt
                                    ).then_inc(const_done, 1)
                for i in range(2):
                    v.memset(z[i][:, :, :], 0.0).then_inc(z_set, 1)
                    v.memset(za[i][:, :, :], 0.0).then_inc(z_set, 1)
                    v.memset(attr[i][:, :, :], 1.0).then_inc(z_set, 1)
                v.wait_ge(z_set, 6)
                for i in range(2):
                    v.memset(z[i][:, :, D + H:D + H + 1], 1.0).then_inc(z_set, 1)
                v.memset(minus_half[:, :], -0.5).then_inc(z_set, 1)
                v.wait_ge(key_t_done, 1)
                v.tensor_copy(key[:, :], bank[0][:, 0:2 * NT]).then_inc(key_done, 1)
                v.wait_ge(w_in, 128)
                v.tensor_tensor(w_src[:, 0, :], w_raw[:, 0, :], w_raw[:, 2, :], ALU.add).then_inc(w_done, 1)
                v.tensor_tensor(w_dst[:, :], w_raw[:, 1, :], w_raw[:, 2, :], ALU.subtract).then_inc(w_done, 1)
                v.wait_ge(w_t, 1)
                v.tensor_copy(wqk_t[:, 0, :], bank[1][:, 0:128]).then_inc(w_tc, 1)
                v.tensor_scalar(wqk_t[:, 1, :], bank[1][:, 128:256], wa[:, 0:1], float(D) ** -0.5,
                                ALU.mult, ALU.mult).then_inc(w_tc, 1)
                v.wait_ge(w_m, 1)
                v.tensor_copy(w_src[:, 1, :], bank[2][:, 0:128]).then_inc(w_done, 1)
                v.wait_ge(const_done, 7)
                v.wait_ge(key_done, 1)

                def count(s, par, k):
                    v.wait_ge(kr_in[par], k * 16 + 16)
                    for a in range(Q):
                        c = (a + 1) * 128
                        t = v.scalar_tensor_tensor(same[par][:, a, 0:c], key_row[par][:, 0:c],
                                                   key[:, bass.ds(s * Q + a, 1)], before[:, a, 0:c],
                                                   ALU.is_equal, ALU.mult,
                                                   accum_out=earlier[:, bass.ds(s * Q + a, 1)])
                    t.then_inc(kr_used, 1)
                steps(v, count, 2 * NS)

                key_v = key[:, :].rearrange("p (s j) -> p s j", j=Q)
                earlier_v = earlier[:, :].rearrange("p (s j) -> p s j", j=Q)
                v.wait_ge(kr_used, 2 * NS)
                v.scalar_tensor_tensor(col_tmp[:, :, :], key_v, -1.0,
                                       spare[:, :].unsqueeze(1).to_broadcast([128, 2 * NS, Q]),
                                       ALU.mult, ALU.add).then_inc(prep_w, 1)
                v.tensor_scalar(earlier[:, :], earlier[:, :], 0.0, None, ALU.is_gt).then_inc(prep_w, 1)
                v.wait_ge(prep_w, 2)
                v.tensor_tensor(col_tmp[:, :, :], col_tmp[:, :, :], earlier_v, ALU.mult).then_inc(prep_w, 1)
                v.wait_ge(prep_w, 3)
                v.tensor_tensor(meta_i[:, :, SC:META], col_tmp[:, :, :], key_v, ALU.add).then_inc(prep_w, 1)
                for d in range(2):
                    o = key_v[:, (1 - d) * NS:(2 - d) * NS, :]
                    v.scalar_tensor_tensor(meta_i[:, d * NS:(d + 1) * NS, 0:Q], o, float(N), o, ALU.is_lt, ALU.mult
                                           ).then_inc(prep_w, 1)
                v.tensor_copy(meta[:, :, KEY:W], key_v).then_inc(prep_w, 1)
                v.tensor_tensor(differ[:, :], key[:, 0:NT], key[:, NT:2 * NT], ALU.not_equal).then_inc(prep_w, 1)
                v.wait_ge(e_in_sem, 32)
                v.wait_ge(prep_w, 8)
                e_v = e_sb[:, :, :].rearrange("p (s j) h -> p s (j h)", j=Q)
                for d in range(2):
                    v.tensor_copy(meta[:, d * NS:(d + 1) * NS, EV:SC], e_v).then_inc(prep_w, 1)
                v.wait_ge(prep_w, 10)
                v.tensor_tensor(e_sb[:, :, :], e_sb[:, :, :], differ[:, :].unsqueeze(2).to_broadcast([128, NT, H]),
                                ALU.mult).then_inc(prep_w, 1)
                v.wait_ge(prep_w, 11)
                for d in range(2):
                    v.tensor_copy(meta[:, d * NS:(d + 1) * NS, W:EV], e_v).then_inc(prep_w, 1)
                v.wait_ge(prep_w, 13)
                v.sem_inc(prep_v, 1)

        early_in = [sem(f"a_early_in{i}") for i in range(2)]
        sc_in = [sem(f"a_sc_in{i}") for i in range(2)]
        row_in = [sem(f"a_row_in{i}") for i in range(2)]
        attr_in = [sem(f"a_attr_in{i}") for i in range(2)]
        x_in = [sem(f"a_x_in{i}") for i in range(2)]
        scat = [sem(f"a_scat{i}") for i in range(2)]
        (turned, turned_sb, mm_done, same_set, mask_set, neg_set, ex_set, act_set, prod_set, logit_set, att_set,
         exp_set, z_ready, r_done, r_copied) = (sem("a_" + n) for n in (
             "turned", "turned_sb", "mm_done", "same_set", "mask_set", "neg_set", "ex_set", "act_set", "prod_set",
             "logit_set", "att_set", "exp_set", "z_ready", "r_done", "r_copied"))
        half_copied, att_put = sem("a_half_copied"), sem("a_att_put")
        t_src, t_dst, t_attr, b_h, b_t = bank[0], bank[1], bank[2], bank[3], bank[4]
        r_bank = [bank[5], bank[6]]

        with nc.Block() as block:
            @block.sync
            def _(sp):
                sp.wait_ge(agg_zeroed, 144)

                def load(s, par, k):
                    again = not (known(k) and k == 0)
                    if again:
                        sp.wait_ge(x_in[par], k * (8 * 16))
                        sp.sem_inc(sp_gate, 1)
                        sp.wait_ge(turned, s - 1)
                        sp.sem_inc(sp_gate, 1)
                        sp.wait_ge(same_set, s - 1)
                        sp.sem_inc(sp_gate, 1)
                        sp.wait_ge(mask_set, s - 1)
                        sp.sem_inc(sp_gate, 1)
                    sp.dma_start(src_row[par][:, :], meta_d[:, bass.ds(s + NS, 1), 0:Q].bitcast(I32)
                                 ).then_inc(early_in[par], 16)
                    sp.dma_start(early[par][:, :], meta_d[:, bass.ds(s, 1), 0:SC]).then_inc(early_in[par], 16)
                    if known(s) and s == NS - 1:
                        sp.dma_start(attr[par][:, 0:Q - 1, 0:EF],
                                     ea_in[s * ST:s * ST + (Q - 1) * 128, 0:EF]
                                     .rearrange("(j p) f -> p j f", p=128)).then_inc(attr_in[par], 16)
                        sp.dma_start(attr[par][:, Q - 1, 0:EF], ea_in[0:128, 0:EF]).then_inc(attr_in[par], 16)
                        sp.wait_ge(attr_in[par], k * 16 + 32)
                        sp.sem_inc(sp_gate, 1)
                        sp.dma_start(attr[par][0:TAIL, Q - 1, 0:EF], ea_in[E - TAIL:E, 0:EF]
                                     ).then_inc(attr_in[par], 16)
                    else:
                        sp.dma_start(attr[par][:, :, 0:EF], ea_in[bass.ds(s * ST, ST), 0:EF]
                                     .rearrange("(j p) f -> p j f", p=128)).then_inc(attr_in[par], 16)
                    sp.dma_start(key_row[par][:, :], key_rows[bass.ds(s * ST, ST)]
                                 .rearrange("(o n) -> o n", o=1).to_broadcast([128, ST])).then_inc(row_in[par], 16)
                    if again:
                        sp.wait_ge(scat[par], k * 64)
                        sp.sem_inc(sp_gate, 1)
                    sp.dma_start(sc_row[par][:, :], meta_d[:, bass.ds(s, 1), SC:META]).then_inc(sc_in[par], 16)
                steps(sp, load, NS)

            @block.gpsimd
            def _(g):
                def scatter(s, par, k):
                    g.wait_ge(sc_in[par], k * 16 + 16)
                    g.sem_inc(pool_gate, 1)
                    g.wait_ge(r_copied, s + 1)
                    g.sem_inc(pool_gate, 1)
                    if not (known(s) and s == 0):
                        g.wait_ge(scat[1 - par], (k + par) * 64)
                    g.sem_inc(pool_gate, 1)
                    for j in range(Q):
                        g.indirect_dma_start(agg[:, :], bass.IndirectOffsetOnAxis(
                            ap=sc_row[par][:, j:j + 1].bitcast(I32), axis=0),
                            summed_a[par][:, j, :], None, compute_op=ALU.add).then_inc(scat[par], 16)

                def step(s, par, k):
                    g.wait_ge(early_in[par], k * 32 + 32)
                    g.sem_inc(pool_gate, 1)
                    if not (known(k) and k == 0):
                        g.wait_ge(turned, s - 1)
                    g.sem_inc(pool_gate, 1)
                    for j in range(Q):
                        g.indirect_dma_start(xs[par][:, j, 0:D], None, x[:, :], bass.IndirectOffsetOnAxis(
                            ap=src_row[par][:, j:j + 1], axis=0)).then_inc(x_in[par], 16)
                        g.indirect_dma_start(xd[par][:, j, :], None, x[:, :], bass.IndirectOffsetOnAxis(
                            ap=early[par][:, j:j + 1].bitcast(I32), axis=0)).then_inc(x_in[par], 16)
                    if not (known(s) and s < 2):
                        scatter(s - 2, par, k - 1)
                steps(g, step, NS, peel=2)
                for s in (NS - 2, NS - 1):
                    scatter(s, s % 2, s // 2)
                for i in range(2):
                    g.wait_ge(scat[i], (NS + 1 - i) // 2 * 64)

            @block.tensor
            def _(pe):
                def add_up(s, par):
                    pe.wait_ge(same_set, s + 1)
                    if not (known(s) and s == 0):
                        pe.wait_ge(r_copied, s)
                    for b in range(Q):
                        for a in range(Q):
                            t = pe.matmul(r_bank[b // 2][:, b % 2 * AW:(b % 2 + 1) * AW],
                                          same[par][:, a, b * 128:(b + 1) * 128], za[par][:, a, :],
                                          start=(a == 0), stop=(a == Q - 1))
                    t.then_inc(r_done, 1)

                def step(s, par, k):
                    pe.wait_ge(x_in[par], k * 128 + 128)
                    if known(s) and s == NS - 1:
                        pe.wait_ge(attr_in[par], k * 16 + 48)
                    else:
                        pe.wait_ge(attr_in[par], k * 16 + 16)
                    for j in range(Q):
                        c = slice(j * 128, (j + 1) * 128)
                        pe.transpose(t_src[:, c], xs[par][:, j, 0:D], ident[:, :])
                        pe.transpose(t_dst[:, c], xd[par][:, j, :], ident[:, :])
                        t = pe.transpose(t_attr[0:EF + 1, c], attr[par][:, j, :], ident[:, :])
                    t.then_inc(turned, 1)
                    pe.wait_ge(turned_sb, s * 3 + 3)
                    if not (known(s) and s == 0):
                        pe.wait_ge(z_ready, s)
                    for j in range(Q):
                        c = slice(j * 128, (j + 1) * 128)
                        pe.matmul(b_h[:, c], xs_t[:, c], w_src[:, 0, :], start=True, stop=False)
                        pe.matmul(b_h[:, c], xd_t[:, c], w_dst[:, :], start=False, stop=False)
                        pe.matmul(b_h[:, c], attr_t[:, c], w_attr[:, :], start=False, stop=True)
                        t = pe.matmul(b_t[:, c], xs_t[:, c], w_src[:, 1, :], start=True, stop=True)
                    t.then_inc(mm_done, 1)
                    if not (known(s) and s == 0):
                        add_up(s - 1, 1 - par)
                steps(pe, step, NS)
                pe.wait_ge(z_ready, NS)
                add_up(NS - 1, (NS - 1) % 2)

            @block.scalar
            def _(act):
                def copy_sums(s, par, k):
                    act.wait_ge(r_done, s + 1)
                    if not (known(k) and k == 0):
                        act.wait_ge(scat[par], k * 64)
                    act.copy(summed_a[par][:, 0:2, :], r_bank[0][:, 0:2 * AW].rearrange("p (j w) -> p j w", j=2)
                             ).then_inc(half_copied, 1)
                    act.wait_ge(half_copied, s + 1)
                    act.copy(summed_a[par][:, 2:4, :], r_bank[1][:, 0:2 * AW].rearrange("p (j w) -> p j w", j=2)
                             ).then_inc(r_copied, 1)

                def step(s, par, k):
                    act.wait_ge(turned, s + 1)
                    if not (known(s) and s == 0):
                        act.wait_ge(mm_done, s)
                    act.copy(xs_t[:, :], t_src[:, :]).then_inc(turned_sb, 1)
                    act.copy(xd_t[:, :], t_dst[:, :]).then_inc(turned_sb, 1)
                    act.copy(attr_t[:, :], t_attr[0:EF + 1, :]).then_inc(turned_sb, 1)
                    act.wait_ge(neg_set, s + 1)
                    act.activation(ex[:, :], neg[:, :], ACT.Exp).then_inc(ex_set, 1)
                    act.wait_ge(logit_set, s * Q + Q)
                    act.activation(att[:, :], logit[:, :], ACT.Tanh).then_inc(att_set, 1)
                    act.wait_ge(att_set, s + 1)
                    act.activation(exp_att[:, :], att[:, :], ACT.Exp).then_inc(exp_set, 1)
                    if not (known(s) and s == 0):
                        copy_sums(s - 1, 1 - par, k - 1 + par)
                steps(act, step, NS, peel=2)
                copy_sums(NS - 1, (NS - 1) % 2, (NS - 1) // 2)

            @block.vector
            def _(v):
                def step(s, par, k):
                    v.wait_ge(attr_in[par], k * 16 + (48 if known(s) and s == NS - 1 else 16))
                    v.tensor_scalar(mask[:, :], attr[par][:, :, 0], 8.0, None, ALU.is_lt).then_inc(mask_set, 1)
                    v.wait_ge(row_in[par], k * 16 + 16)
                    v.wait_ge(early_in[par], k * 32 + 32)
                    if not (known(k) and k == 0):
                        v.wait_ge(r_done, s - 1)
                    for a in range(Q):
                        t = v.tensor_scalar(same[par][:, a, :], key_row[par][:, :], early[par][:, KEY + a:KEY + a + 1],
                                            None, ALU.is_equal)
                    t.then_inc(same_set, 1)
                    v.wait_ge(mm_done, s + 1)
                    v.tensor_scalar(neg[:, :], b_h[:, :], 0.0, None, ALU.min).then_inc(neg_set, 1)
                    v.wait_ge(ex_set, s + 1)
                    v.scalar_tensor_tensor(act_f[:, :], b_h[:, :], 0.0, ex[:, :], ALU.max, ALU.add
                                           ).then_inc(act_set, 1)
                    v.wait_ge(act_set, s * (Q + 1) + 1)
                    v.wait_ge(mask_set, s + 1)
                    for j in range(Q):
                        c = slice(j * 128, (j + 1) * 128)
                        v.tensor_scalar(act_f[:, c], act_f[:, c], -1.0, mask[:, j:j + 1], ALU.add, ALU.mult
                                        ).then_inc(act_set, 1)
                    v.wait_ge(act_set, s * (Q + 1) + Q + 1)
                    for j in range(Q):
                        c = slice(j * 128, (j + 1) * 128)
                        v.tensor_tensor_reduce(prod[:, c], b_t[:, c], act_f[:, c], 1.0, 0.0, ALU.mult, ALU.add,
                                               logit[:, j:j + 1]).then_inc(logit_set, 1)
                    v.wait_ge(exp_set, s + 1)
                    v.tensor_copy(za[par][:, :, D], att[:, :]).then_inc(att_put, 1)
                    v.wait_ge(att_put, s + 1)
                    v.tensor_tensor(za[par][:, :, 0:D], act_f[:, :].rearrange("p (j f) -> p j f", j=Q),
                                    exp_att[:, :].unsqueeze(2).to_broadcast([128, Q, D]), ALU.mult
                                    ).then_inc(z_ready, 1)
                steps(v, step, NS)

        def shape(s):
            return (NREST, 1) if known(s) and s == NCH else (128, R)

        def chunk(a, s, w):
            if known(s) and s == NCH:
                return a[NMAIN:N, 0:w].rearrange("(p r) f -> p r f", r=1)
            v = a[0:NMAIN, 0:w].rearrange("(p c r) f -> p c r f", p=128, r=R)[:, bass.ds(s, 1), :, :]
            return v.rearrange("p c r f -> p (c r) f")

        def layernorm(tag, write_to):
            stat_set, mv_set, gate, eps_set, root_set, normed_set = (sem(tag + n) for n in (
                "stat_set", "mv_set", "v_gate", "eps_set", "root_set", "normed_set"))
            written = [sem(f"{tag}written{i}") for i in range(2)]

            def sums(v, s, par, res_set, res_value):
                P, RR = shape(s)
                v.wait_ge(res_set, res_value)
                for r in range(RR):
                    t = v.bn_stats(stats[0:P, r, :], res[par][0:P, r, :])
                t.then_inc(stat_set, 1)
                v.wait_ge(stat_set, s + 1)
                if not (known(s) and s < 2):
                    v.wait_ge(eps_set, s - 1)
                v.sem_inc(gate, 1)
                for r in range(RR):
                    t = v.bn_aggr(mv[par][0:P, r, :], stats[0:P, r, :])
                t.then_inc(mv_set, 1)

            def root(g, s, par):
                P, RR = shape(s)
                g.wait_ge(mv_set, s + 1)
                g.sem_inc(pool_gate, 1)
                if not (known(s) and s < 2):
                    g.wait_ge(normed_set, s - 1)
                g.sem_inc(pool_gate, 1)
                g.tensor_scalar(rstd[par][0:P, 0:RR], mv[par][0:P, 0:RR, 1], EPS, None, ALU.add).then_inc(eps_set, 1)
                g.wait_ge(eps_set, s + 1)
                g.sem_inc(pool_gate, 1)
                g.tensor_tensor(rstd[par][0:P, 0:RR], rstd[par][0:P, 0:RR], minus_half[0:P, 0:RR], ALU.pow
                                ).then_inc(root_set, 1)

            def scale(v, s, par, uses):
                P, RR = shape(s)
                v.wait_ge(root_set, s + 1)
                if not (known(s) and s < 2):
                    v.wait_ge(written[par], uses * 16)
                for r in range(RR):
                    t = v.tensor_scalar(normed[par][0:P, r, :], res[par][0:P, r, :], mv[par][0:P, r, 0:1],
                                        rstd[par][0:P, r:r + 1], ALU.subtract, ALU.mult)
                t.then_inc(normed_set, 1)

            def write(sp, s, par):
                P, RR = shape(s)
                sp.wait_ge(normed_set, s + 1)
                sp.sem_inc(sp_gate, 1)
                sp.dma_start(chunk(write_to, s, D), normed[par][0:P, 0:RR, :]).then_inc(written[par], 16)

            return sums, root, scale, write, normed_set, written

        chunk_in = [sem(f"n_chunk_in{i}") for i in range(4)]
        xa_t_half = sem("n_xa_t_half")
        decay_set, xa_set, xa_turned, xa_t_set, node_mm, res_set = (sem("n_" + n) for n in (
            "decay_set", "xa_set", "xa_turned", "xa_t_set", "node_mm", "res_set"))
        sums, root, scale, write, normed_set, written = layernorm("n_", x1)

        def uses(s, slot, k):
            return k * 2 + slot // 2

        with nc.Block() as block:
            @block.sync
            def _(sp):
                def step(s, slot, k):
                    P, RR = shape(s)
                    if not (known(k) and k == 0):
                        sp.wait_ge(res_set, s - 3)
                        sp.sem_inc(sp_gate, 1)
                    sp.dma_start(xc[slot][0:P, 0:RR, :], chunk(x, s, D)).then_inc(chunk_in[slot], 16)
                    sp.dma_start(agc[slot][0:P, 0:RR, :], chunk(agg, s, AW)).then_inc(chunk_in[slot], 16)
                    if not (known(s) and s < 3):
                        write(sp, s - 3, (slot - 3) % 2)
                steps(sp, step, NCH + 1, 4)
                for s in range(NCH - 2, NCH + 1):
                    write(sp, s, s % 2)
                for i in range(2):
                    sp.wait_ge(written[i], (NCH + 2 - i) // 2 * 16)

            @block.gpsimd
            def _(g):
                steps(g, lambda s, slot, k: root(g, s, slot % 2), NCH + 1, 4)

            @block.scalar
            def _(act):
                def step(s, slot, k):
                    P, RR = shape(s)
                    act.wait_ge(chunk_in[slot], k * 32 + 32)
                    act.activation(decay[0:P, slot, 0:RR], agc[slot][0:P, 0:RR, D], ACT.Exp, scale=-1.0
                                   ).then_inc(decay_set, 1)
                    act.wait_ge(xa_turned, s + 1)
                    if not (known(s) and s == 0):
                        act.wait_ge(node_mm, s)
                    b = 4 * (slot % 2)
                    for h in range(-(-RR // 4)):
                        c = min(RR - 4 * h, 4) * 128
                        t = act.copy(xa_t[:, h * 512:h * 512 + c], bank[b + h][:, 0:c])
                        t.then_inc(xa_t_half, 1)
                    act.wait_ge(xa_t_half, s * 2 + 2 if not (known(s) and s == NCH) else s * 2 + 1)
                    act.sem_inc(xa_t_set, 1)
                steps(act, step, NCH + 1, 4)

            @block.tensor
            def _(pe):
                def step(s, slot, k):
                    P, RR = shape(s)
                    b = 4 * (slot % 2)
                    pe.wait_ge(xa_set, s + 1)
                    for r in range(RR):
                        t = pe.transpose(bank[b + r // 4][:, r % 4 * 128:r % 4 * 128 + P], xa[0:P, r, :],
                                         ident[0:P, 0:P])
                    t.then_inc(xa_turned, 1)
                    pe.wait_ge(xa_t_set, s + 1)
                    if not (known(s) and s < 2):
                        pe.wait_ge(res_set, s - 1)
                    for r in range(RR):
                        o = bank[b + 2 + r // 4][0:P, r % 4 * 128:r % 4 * 128 + 128]
                        pe.matmul(o, xa_t[:, r * 128:r * 128 + P], wu[:, :], start=True, stop=False)
                        t = pe.matmul(o, ones[:, 0:P], bu_row[:, :], start=False, stop=True)
                    t.then_inc(node_mm, 1)
                steps(pe, step, NCH + 1, 4)

            @block.vector
            def _(v):
                def make_xa(s, slot, k):
                    P, RR = shape(s)
                    v.wait_ge(decay_set, s + 1)
                    if not (known(s) and s == 0):
                        v.wait_ge(xa_turned, s)
                    for r in range(RR):
                        t = v.scalar_tensor_tensor(xa[0:P, r, :], agc[slot][0:P, r, 0:D],
                                                   decay[0:P, slot, r:r + 1], xc[slot][0:P, r, :],
                                                   ALU.mult, ALU.add)
                    t.then_inc(xa_set, 1)

                def make_res(s, slot, k):
                    P, RR = shape(s)
                    b = 4 * (slot % 2)
                    v.wait_ge(node_mm, s + 1)
                    for h in range(-(-RR // 4)):
                        c = min(RR - 4 * h, 4)
                        t = v.tensor_tensor(res[slot % 2][0:P, 4 * h:4 * h + c, :], xc[slot][0:P, 4 * h:4 * h + c, :],
                                            bank[b + 2 + h][0:P, 0:c * 128].rearrange("p (r f) -> p r f", f=128),
                                            ALU.add)
                    t.then_inc(res_set, 1)
                    sums(v, s, slot % 2, res_set, s + 1)

                def step(s, slot, k):
                    make_xa(s, slot, k)
                    if not (known(s) and s < 2):
                        sl, kk = back(slot, k, 2, 4)
                        scale(v, s - 2, sl % 2, uses(s - 2, sl, kk))
                    if not (known(s) and s < 1):
                        make_res(s - 1, *back(slot, k, 1, 4))
                steps(v, step, NCH + 1, 4)
                scale(v, NCH - 1, (NCH - 1) % 2, (NCH - 1) // 2)
                make_res(NCH, NCH % 4, NCH // 4)
                scale(v, NCH, NCH % 2, NCH // 2)

        NH = 2 * NS
        early_in = [sem(f"h_early_in{i}") for i in range(2)]
        sc_in = [sem(f"h_sc_in{i}") for i in range(2)]
        row_in = [sem(f"h_row_in{i}") for i in range(2)]
        v_in = [sem(f"h_v_in{i}") for i in range(2)]
        scat = [sem(f"h_scat{i}") for i in range(2)]
        same_set, e_put, inv_set, wn_set, z_ready, r_done, half_copied, r_copied, z_cleared = (sem("h_" + n) for n in (
            "same_set", "e_put", "inv_set", "wn_set", "z_ready", "r_done", "half_copied", "r_copied", "z_cleared"))

        def hop(h):
            source = x1 if h == 0 else u[h - 1]
            width = D if h == 0 else UW
            target = u[h] if h < 3 else u[1]
            share = 1.0 if h < 3 else 1.0 / 12
            base, kb = h * NH, h * (NH // 2)

            with nc.Block() as block:
                @block.sync
                def _(sp):
                    if h == 0:
                        sp.wait_ge(u_zeroed, 27 * 16)

                    def load(s, par, k):
                        again = not (known(k) and k == 0)
                        if again:
                            sp.wait_ge(v_in[par], (k + kb) * 64)
                            sp.sem_inc(sp_gate, 1)
                            sp.wait_ge(same_set, s - 1 + base)
                            sp.sem_inc(sp_gate, 1)
                            sp.wait_ge(z_ready, s - 1 + base)
                            sp.sem_inc(sp_gate, 1)
                            if h < 3:
                                sp.wait_ge(e_put, s - 1 + base)
                            sp.sem_inc(sp_gate, 1)
                        sp.dma_start(early[par][:, :], meta_d[:, bass.ds(s, 1), 0:SC]).then_inc(early_in[par], 16)
                        sp.dma_start(key_row[par][:, :], key_rows[bass.ds(s * ST, ST)]
                                     .rearrange("(o n) -> o n", o=1).to_broadcast([128, ST])).then_inc(row_in[par], 16)
                        if again:
                            sp.wait_ge(scat[par], (k + kb) * 64)
                            sp.sem_inc(sp_gate, 1)
                        sp.dma_start(sc_row[par][:, :], meta_d[:, bass.ds(s, 1), SC:META]).then_inc(sc_in[par], 16)
                    steps(sp, load, NH)

                @block.gpsimd
                def _(g):
                    def scatter(s, par, k):
                        g.wait_ge(sc_in[par], (k + kb) * 16 + 16)
                        g.sem_inc(pool_gate, 1)
                        g.wait_ge(r_copied, s + 1 + base)
                        g.sem_inc(pool_gate, 1)
                        if not (known(s) and s == 0):
                            g.wait_ge(scat[1 - par], (k + kb + par) * 64)
                        g.sem_inc(pool_gate, 1)
                        for j in range(Q):
                            g.indirect_dma_start(target[:, :], bass.IndirectOffsetOnAxis(
                                ap=sc_row[par][:, j:j + 1].bitcast(I32), axis=0),
                                summed[par][:, j, :], None, compute_op=ALU.add).then_inc(scat[par], 16)

                    def step(s, par, k):
                        g.wait_ge(early_in[par], (k + kb) * 16 + 16)
                        g.sem_inc(pool_gate, 1)
                        if not (known(k) and k == 0):
                            g.wait_ge(z_ready, s - 1 + base)
                        g.sem_inc(pool_gate, 1)
                        for j in range(Q):
                            g.indirect_dma_start(xs[par][:, j, 0:width], None, source[:, :],
                                                 bass.IndirectOffsetOnAxis(
                                ap=early[par][:, j:j + 1].bitcast(I32), axis=0)).then_inc(v_in[par], 16)
                        if not (known(s) and s < 2):
                            scatter(s - 2, par, k - 1)
                    steps(g, step, NH, peel=2)
                    for s in (NH - 2, NH - 1):
                        scatter(s, s % 2, s // 2)
                    for i in range(2):
                        g.wait_ge(scat[i], (h + 1) * (NH // 2) * 64)

                @block.tensor
                def _(pe):
                    def step(s, par, k):
                        pe.wait_ge(same_set, s + 1 + base)
                        pe.wait_ge(z_ready, s + 1 + base)
                        if h < 3:
                            pe.wait_ge(e_put, s + 1 + base)
                        if not (known(s) and s < 2):
                            pe.wait_ge(r_copied, s - 1 + base)
                        for b in range(Q):
                            for a in range(Q):
                                t = pe.matmul(bank[2 * par + b // 2][:, b % 2 * UW:(b % 2 + 1) * UW],
                                              same[par][:, a, b * 128:(b + 1) * 128], z[par][:, a, :],
                                              start=(a == 0), stop=(a == Q - 1))
                        t.then_inc(r_done, 1)
                    steps(pe, step, NH)

                @block.scalar
                def _(act):
                    def copy_sums(s, par, k):
                        act.wait_ge(r_done, s + 1 + base)
                        if not (known(k) and k == 0):
                            act.wait_ge(scat[par], (k + kb) * 64)
                        for i in range(2):
                            act.copy(summed[par][:, 2 * i:2 * i + 2, :],
                                     bank[2 * par + i][:, 0:2 * UW].rearrange("p (j w) -> p j w", j=2)
                                     ).then_inc(half_copied, 1)
                        act.wait_ge(half_copied, s * 2 + 2 + 2 * base)
                        act.sem_inc(r_copied, 1)

                    def step(s, par, k):
                        if h < 3:
                            act.wait_ge(early_in[par], (k + kb) * 16 + 16)
                            if not (known(s) and s < 2):
                                act.wait_ge(r_done, s - 1 + base)
                            act.copy(z[par][:, :, D:D + H],
                                     early[par][:, EV:SC].rearrange("p (j h) -> p j h", j=Q)).then_inc(e_put, 1)
                        if not (known(s) and s < 1):
                            copy_sums(s - 1, *back(par, k, 1, 2))
                    steps(act, step, NH)
                    copy_sums(NH - 1, 1, NH // 2 - 1)

                @block.vector
                def _(v):
                    if h == 3:
                        for i in range(2):
                            v.memset(z[i][:, :, D:D + H + 1], 0.0).then_inc(z_cleared, 1)
                        v.wait_ge(z_cleared, 2)

                    def step(s, par, k):
                        v.wait_ge(row_in[par], (k + kb) * 16 + 16)
                        v.wait_ge(early_in[par], (k + kb) * 16 + 16)
                        if not (known(s) and s < 2):
                            v.wait_ge(r_done, s - 1 + base)
                        for a in range(Q):
                            t = v.tensor_scalar(same[par][:, a, :], key_row[par][:, :],
                                                early[par][:, KEY + a:KEY + a + 1], None, ALU.is_equal)
                        t.then_inc(same_set, 1)
                        v.wait_ge(v_in[par], (k + kb) * 64 + 64)
                        weight = early[par][:, W:EV].rearrange("p (j h) -> p j h", j=Q)
                        if h > 0:
                            sum_e = xs[par][:, :, D:D + H]
                            v.scalar_tensor_tensor(inv[:, :, :], sum_e, 0.0, sum_e, ALU.is_equal, ALU.add
                                                   ).then_inc(inv_set, 1)
                            v.wait_ge(inv_set, (s + base - NH) * 2 + 1)
                            v.reciprocal(inv[:, :, :], inv[:, :, :]).then_inc(inv_set, 1)
                            v.wait_ge(inv_set, (s + base - NH) * 2 + 2)
                            v.scalar_tensor_tensor(wn[:, :, :], weight, share, inv[:, :, :], ALU.mult, ALU.mult
                                                   ).then_inc(wn_set, 1)
                            v.wait_ge(wn_set, s + 1 + base - NH)
                            weight = wn[:, :, :]
                        for j in range(Q):
                            t = v.tensor_tensor(z[par][:, j, 0:D].rearrange("p (h f) -> p h f", h=H),
                                                xs[par][:, j, 0:D].rearrange("p (h f) -> p h f", h=H),
                                                weight[:, j, :].unsqueeze(2).to_broadcast([128, H, HF]), ALU.mult)
                        t.then_inc(z_ready, 1)
                    steps(v, step, NH)

        for h in range(4):
            hop(h)

        chunk_in = [sem(f"o_chunk_in{i}") for i in range(4)]
        b_set, res_set = sem("o_b_set"), sem("o_res_set")
        sums, root, scale, write, normed_set, written = layernorm("o_", out)

        with nc.Block() as block:
            @block.sync
            def _(sp):
                def step(s, slot, k):
                    P, RR = shape(s)
                    if not (known(k) and k == 0):
                        sp.wait_ge(res_set, s - 3)
                        sp.sem_inc(sp_gate, 1)
                    sp.dma_start(xc[slot][0:P, 0:RR, :], chunk(x1, s, D)).then_inc(chunk_in[slot], 16)
                    for i in range(3):
                        sp.dma_start(uc[i][slot][0:P, 0:RR, :], chunk(u[i], s, UW)).then_inc(chunk_in[slot], 16)
                    if not (known(s) and s < 3):
                        write(sp, s - 3, (slot - 3) % 2)
                steps(sp, step, NCH + 1, 4)
                for s in range(NCH - 2, NCH + 1):
                    write(sp, s, s % 2)
                for i in range(2):
                    sp.wait_ge(written[i], (NCH + 2 - i) // 2 * 16)

            @block.gpsimd
            def _(g):
                steps(g, lambda s, slot, k: root(g, s, slot % 2), NCH + 1, 4)

            @block.vector
            def _(v):
                B = 7

                def make_res(s, slot, k):
                    P, RR = shape(s)
                    u0, u1, u2 = (uc[i][slot][0:P, 0:RR, :] for i in range(3))
                    iso, ci = isolated[0:P, 0:RR], cinv[0:P, 0:RR, :]
                    v.wait_ge(chunk_in[slot], k * 64 + 64)
                    v.tensor_scalar(iso, u0[:, :, D + H], 0.0, None, ALU.is_equal).then_inc(b_set, 1)
                    v.wait_ge(b_set, s * B + 1)
                    v.tensor_tensor(ci, u0[:, :, D:D + H], iso.unsqueeze(2).to_broadcast([P, RR, H]), ALU.add
                                    ).then_inc(b_set, 1)
                    v.scalar_tensor_tensor(u0[:, :, 0:D], u1[:, :, 0:D], 0.5, u0[:, :, 0:D], ALU.mult, ALU.add
                                           ).then_inc(b_set, 1)
                    v.wait_ge(b_set, s * B + 3)
                    v.reciprocal(ci, ci).then_inc(b_set, 1)
                    v.scalar_tensor_tensor(u0[:, :, 0:D], u2[:, :, 0:D], 1.0 / 6, u0[:, :, 0:D], ALU.mult, ALU.add
                                           ).then_inc(b_set, 1)
                    v.wait_ge(b_set, s * B + 5)
                    for r in range(RR):
                        t = v.tensor_tensor(u0[:, r, 0:D].rearrange("p (h f) -> p h f", h=H),
                                            u0[:, r, 0:D].rearrange("p (h f) -> p h f", h=H),
                                            ci[:, r, :].unsqueeze(2).to_broadcast([P, H, HF]), ALU.mult)
                    t.then_inc(b_set, 1)
                    v.wait_ge(b_set, s * B + 6)
                    if not (known(s) and s < 2):
                        v.wait_ge(normed_set, s - 1)
                    v.scalar_tensor_tensor(res[slot % 2][0:P, 0:RR, :], xc[slot][0:P, 0:RR, :], 2.0, u0[:, :, 0:D],
                                           ALU.mult, ALU.add).then_inc(res_set, 1)
                    v.sem_inc(b_set, 1)
                    sums(v, s, slot % 2, res_set, s + 1)

                def step(s, slot, k):
                    make_res(s, slot, k)
                    if not (known(s) and s < 1):
                        sl, kk = back(slot, k, 1, 4)
                        scale(v, s - 1, sl % 2, uses(s - 1, sl, kk))
                steps(v, step, NCH + 1, 4)
                scale(v, NCH, NCH % 2, NCH // 2)


_INS = ['x', 'src', 'dst', 'edge_attr3_4x1', 'edge_attr_70', 'L0_gnn_Wf', 'L0_gnn_bf', 'L0_gnn_Wq', 'L0_gnn_Wk',
        'L0_gnn_Wa', 'L0_gnn_Wu', 'L0_gnn_bu']


def kernel(**inputs):
    import numpy as _np
    import concourse.bacc as _bacc
    from concourse import mybir as _mybir
    from concourse.bass_utils import run_bass_kernel_spmd as _run

    nc = _bacc.Bacc("TRN2", target_bir_lowering=False, num_devices=1)
    arrays, args = {}, []
    for name in _INS:
        a = _np.ascontiguousarray(inputs[name])
        arrays[f"in_{name}_dram"] = a
        args.append(nc.dram_tensor(f"in_{name}_dram", a.shape, _mybir.dt.from_np(a.dtype), kind="ExternalInput").ap())
    args.append(nc.dram_tensor("out_0_dram", (N, D), _mybir.dt.float32, kind="ExternalOutput").ap())
    build(nc, *args)
    r = _run(nc, [arrays], core_ids=[0])
    return r.results[0]["out_0_dram"]
```

```python
from contextlib import ExitStack

import concourse.bass as bass
from concourse import mybir

F32 = mybir.dt.float32
I32 = mybir.dt.int32
ALU = mybir.AluOpType
ACT = mybir.ActivationFunctionType
AX = mybir.AxisListType

N = 50000
E = 25000
D = 128
H = 4
HF = D // H
EF = 65
EC = 70
Q = 4
ST = Q * 128
NS = -(-E // ST)
NT = NS * Q
NP = NT * 128
KC = 7
HALF = NT // 2
TAIL = E - (NT - 1) * 128
ZP, ZR = 48, 11
ROWS = 2 * NS * ZP * ZR
assert ROWS >= N + ST
AW = D + 4
UW = D + 8
KEY, W, EV, SC = Q, 2 * Q, 2 * Q + Q * H, 2 * Q + 2 * Q * H
META = SC + Q
R = 6
NCH = (N // 128) // R
NMAIN = NCH * R * 128
NREST = N - NMAIN
EPS = 1e-5


def steps(eng, body, n, m=2, peel=1):
    for s in range(m * peel):
        body(s, s % m, s // m)
    with eng.Fori(peel, n // m) as k:
        for i in range(m):
            body(k * m + i, i, k)
    for s in range(n // m * m, n):
        body(s, s % m, s // m)


def back(slot, k, d, m):
    return (slot - d) % m, k - (1 if slot < d else 0)


def known(s):
    return isinstance(s, int)


def build(nc, x, src, dst, e_in, ea_in, Wf, bf, Wq, Wk, Wa, Wu, bu, out):
    key_rows = nc.dram_tensor("key_rows", (2 * NP,), I32).ap()
    meta_d = nc.dram_tensor("meta_d", (128, 2 * NS, META), F32).ap()
    agg = nc.dram_tensor("agg", (ROWS, AW), F32).ap()
    x1 = nc.dram_tensor("x1", (N, D), F32).ap()
    u = [nc.dram_tensor(f"u{i}", (ROWS, UW), F32).ap() for i in range(3)]

    with ExitStack() as ctx:
        def sb(name, shape, dt=F32):
            return ctx.enter_context(nc.sbuf_tensor(name, shape, dt))

        def sem(name):
            return ctx.enter_context(nc.semaphore(name))

        bank = [ctx.enter_context(nc.psum_tensor(f"bank{i}", [128, 512], F32)) for i in range(8)]

        ident = sb("ident", [128, 128])
        pos_i = sb("pos_i", [128, ST], I32)
        part_i = sb("part_i", [128, Q], I32)
        pos = sb("pos", [128, ST])
        part = sb("part", [128, Q])
        before = sb("before", [128, Q, ST])
        spare = sb("spare", [128, Q])
        zero = sb("zero", [2 * ZP, ZR * UW])
        minus_half = sb("minus_half", [128, R])
        rows_i = sb("rows_i", [HALF, 2, 2, 128], I32)
        rows_f = sb("rows_f", [HALF, 4, 128])
        key = sb("key", [128, 2 * NT])
        e_sb = sb("e_sb", [128, NT, H])
        differ = sb("differ", [128, NT])
        earlier = sb("earlier", [128, 2 * NT])
        col_tmp = sb("col_tmp", [128, 2 * NS, Q])
        meta = sb("meta", [128, 2 * NS, META])
        meta_i = meta[:, :, :].bitcast(I32)
        key_rows_sb = [sb(f"key_rows_sb{i}", [128, KC * ST], I32) for i in range(2)]
        key_row = [sb(f"key_row{i}", [128, ST], I32) for i in range(2)]
        same = [sb(f"same{i}", [128, Q, ST]) for i in range(2)]
        w_raw = sb("w_raw", [128, 3, D])
        w_attr = sb("w_attr", [EF + 1, D])
        w_src = sb("w_src", [128, 2, D])
        w_dst = sb("w_dst", [128, D])
        wqk = sb("wqk", [128, 2, D])
        wqk_t = sb("wqk_t", [128, 2, D])
        wa = sb("wa", [128, 1])
        wu = sb("wu", [128, D])
        bu_all = sb("bu_all", [128, D])
        src_row = [sb(f"src_row{i}", [128, Q], I32) for i in range(2)]
        early = [sb(f"early{i}", [128, SC]) for i in range(2)]
        sc_row = [sb(f"sc_row{i}", [128, Q]) for i in range(2)]
        xs = [sb(f"xs{i}", [128, Q, UW]) for i in range(2)]
        xd = [sb(f"xd{i}", [128, Q, D]) for i in range(2)]
        attr = [sb(f"attr{i}", [128, Q, EF + 1]) for i in range(2)]
        xs_t = sb("xs_t", [128, ST])
        xd_t = sb("xd_t", [128, ST])
        attr_t = sb("attr_t", [EF + 1, ST])
        neg = sb("neg", [128, ST])
        ex = sb("ex", [128, ST])
        act_f = sb("act_f", [128, ST])
        prod = sb("prod", [128, ST])
        mask = sb("mask", [128, Q])
        logit = sb("logit", [128, Q])
        att = sb("att", [128, Q])
        exp_att = sb("exp_att", [128, Q])
        z = [sb(f"z{i}", [128, Q, UW]) for i in range(2)]
        za = [sb(f"za{i}", [128, Q, AW]) for i in range(2)]
        summed = [sb(f"summed{i}", [128, Q, UW]) for i in range(2)]
        summed_a = [sb(f"summed_a{i}", [128, Q, AW]) for i in range(2)]
        inv = sb("inv", [128, Q, H])
        wn = sb("wn", [128, Q, H])
        xc = [sb(f"xc{i}", [128, R, D]) for i in range(4)]
        uc = [[sb(f"uc{j}_{i}", [128, R, UW]) for i in range(4)] for j in range(3)]
        agc = [uc[0][i][:, :, 0:AW] for i in range(4)]
        decay = sb("decay", [128, 4, R])
        xa = sb("xa", [128, R, D])
        xa_t = sb("xa_t", [128, R * 128])
        res = [sb(f"res{i}", [128, R, D]) for i in range(2)]
        stats = sb("stats", [128, R, 6])
        mv = [sb(f"mv{i}", [128, R, 2]) for i in range(2)]
        rstd = [sb(f"rstd{i}", [128, R]) for i in range(2)]
        shift = [sb(f"shift{i}", [128, R]) for i in range(2)]
        normed = [same[i][:, :, :].rearrange("p q c -> p (q c)")[:, 0:R * D].rearrange("p (r f) -> p r f", r=R)
                  for i in range(2)]
        cinv = sb("cinv", [128, R, H])
        isolated = sb("isolated", [128, R])

        iota_done, pads_set, rows_in, e_in_sem, w_in, w_in2 = (sem(n) for n in (
            "iota_done", "pads_set", "rows_in", "e_in", "w_in", "w_in2"))
        const_done, zero_done, rows_f_done, key_t_done, key_done = (sem(n) for n in (
            "const_done", "zero_done", "rows_f_done", "key_t_done", "key_done"))
        key_rows_out, meta_out, agg_zeroed, prep_v, w_t, w_tc, w_m, w_done, e_zero = (sem(n) for n in (
            "key_rows_out", "meta_out", "agg_zeroed", "prep_v", "w_t", "w_tc", "w_m", "w_done",
            "e_zero"))
        kr_in = [sem(f"p_kr_in{i}") for i in range(2)]
        kr_used = sem("p_kr_used")
        counted = sem("counted")
        sc_set = [sem(f"sc_set{d}") for d in range(2)]
        u_zeroed = [sem(f"u_zeroed{i}") for i in range(3)]
        prep_c, prep_w, z_set = sem("prep_c"), sem("prep_w"), sem("z_set")
        sp_gate, pool_gate = sem("sp_gate"), sem("pool_gate")

        key_v = key[:, :].rearrange("p (s j) -> p s j", j=Q)
        earlier_v = earlier[:, :].rearrange("p (s j) -> p s j", j=Q)

        def put_scatter_rows(v, d):
            t, n = slice(d * NS, (d + 1) * NS), slice(d * NT, (d + 1) * NT)
            v.scalar_tensor_tensor(col_tmp[:, t, :], key_v[:, t, :], -1.0,
                                   spare[:, :].unsqueeze(1).to_broadcast([128, NS, Q]),
                                   ALU.mult, ALU.add).then_inc(sc_set[d], 1)
            v.tensor_scalar(earlier[:, n], earlier[:, n], 0.0, None, ALU.is_gt).then_inc(sc_set[d], 1)
            v.wait_ge(sc_set[d], 2)
            v.tensor_tensor(col_tmp[:, t, :], col_tmp[:, t, :], earlier_v[:, t, :], ALU.mult).then_inc(sc_set[d], 1)
            v.wait_ge(sc_set[d], 3)
            v.tensor_tensor(meta_i[:, t, SC:META], col_tmp[:, t, :], key_v[:, t, :], ALU.add).then_inc(sc_set[d], 1)

        def zero_rows(a, s, p):
            return a[bass.ds(s * (p * ZR), p * ZR), :].rearrange("(p r) w -> p (r w)", p=p)

        with nc.Block() as block:
            @block.gpsimd
            def _(g):
                g.iota(pos_i[:, :], [[1, ST]], base=0, channel_multiplier=0).then_inc(iota_done, 1)
                g.iota(part_i[:, :], [[128, Q]], base=0, channel_multiplier=1).then_inc(iota_done, 1)
                for d in range(2):
                    g.iota(rows_i[:, d, 1, :], [[1, 128]], base=N + (Q - 1) * 128,
                           channel_multiplier=0).then_inc(pads_set, 1)

            @block.sync
            def _(sp):
                sp.dma_start(w_raw[:, :, :], Wf[0:3 * D, :].rearrange("(k p) n -> p k n", p=128)).then_inc(w_in, 16)
                sp.dma_start(w_attr[0:EF, :], Wf[3 * D:3 * D + EF, :]).then_inc(w_in, 16)
                sp.dma_start(w_attr[EF:EF + 1, :], bf.rearrange("(o n) -> o n", o=1)).then_inc(w_in, 16)
                sp.dma_start(wqk[:, 0, :], Wq[:, :]).then_inc(w_in, 16)
                sp.dma_start(wqk[:, 1, :], Wk[:, :]).then_inc(w_in, 16)
                sp.dma_start(wa[:, :], Wa[:, :]).then_inc(w_in, 16)
                sp.dma_start(wu[:, :], Wu[:, :]).then_inc(w_in, 16)
                sp.dma_start(bu_all[:, :], bu.rearrange("(o n) -> o n", o=1).to_broadcast([128, D])).then_inc(w_in, 16)
                sp.wait_ge(pads_set, 2)
                first = HALF * 128
                for d, ends in enumerate((src, dst)):
                    sp.dma_start(rows_i[:, d, 0, :], ends[0:first].rearrange("(r c) -> r c", c=128)
                                 ).then_inc(rows_in, 16)
                    sp.dma_start(rows_i[0:HALF - 1, d, 1, :],
                                 ends[first:first + (HALF - 1) * 128].rearrange("(r c) -> r c", c=128)
                                 ).then_inc(rows_in, 16)
                    sp.dma_start(rows_i[HALF - 1:HALF, d, 1, 0:TAIL],
                                 ends[E - TAIL:E].rearrange("(o n) -> o n", o=1)).then_inc(rows_in, 16)
                sp.wait_ge(rows_in, 96)
                for d in range(2):
                    for h in range(2):
                        sp.dma_start(key_rows[(2 * d + h) * first:(2 * d + h + 1) * first]
                                     .rearrange("(r c) -> r c", c=128), rows_i[:, d, h, :]).then_inc(key_rows_out, 16)
                sp.wait_ge(key_rows_out, 64)

                def load_keys(s, par, k):
                    if not (known(k) and k == 0):
                        sp.wait_ge(kr_used, s - 1)
                        sp.sem_inc(sp_gate, 1)
                    sp.dma_start(key_rows_sb[par][:, :], key_rows[bass.ds(s * KC * ST, KC * ST)]
                                 .rearrange("(o n) -> o n", o=1).to_broadcast([128, KC * ST])
                                 ).then_inc(kr_in[par], 16)
                load_keys(0, 0, 0)
                load_keys(1, 1, 0)
                sp.wait_ge(e_zero, 1)
                sp.dma_start(e_sb[:, 0:NT - 1, :], e_in[0:E - TAIL, :, 0].rearrange("(t p) h -> p t h", p=128)
                             ).then_inc(e_in_sem, 16)
                sp.dma_start(e_sb[0:TAIL, NT - 1, :], e_in[E - TAIL:E, :, 0]).then_inc(e_in_sem, 16)
                with sp.Fori(1, NS // KC // 2) as k:
                    load_keys(k * 2, 0, k)
                    load_keys(k * 2 + 1, 1, k)
                load_keys(NS // KC - 1, 0, NS // KC // 2)
                sp.wait_ge(prep_v, 1)
                sp.dma_start(meta_d[:, 0:NS, :], meta[:, 0:NS, :]).then_inc(meta_out, 16)
                sp.dma_start(meta_d[:, NS:2 * NS, 0:SC], meta[:, NS:2 * NS, 0:SC]).then_inc(meta_out, 16)
                sp.wait_ge(meta_out, 32)

            @block.scalar
            def _(act):
                act.wait_ge(zero_done, 1)
                act.wait_ge(kr_in[1], 16)
                with act.Fori(0, NS) as s:
                    act.dma_start(zero_rows(agg, s, 2 * ZP), zero[:, 0:ZR * AW]).then_inc(agg_zeroed, 16)

            @block.tensor
            def _(pe):
                pe.wait_ge(rows_f_done, 1)
                pe.wait_ge(const_done, 1)
                for i in range(4):
                    t = pe.transpose(bank[0][:, i * HALF:(i + 1) * HALF], rows_f[:, i, :], ident[0:HALF, 0:HALF])
                t.then_inc(key_t_done, 1)
                pe.wait_ge(w_in, 128)
                pe.transpose(bank[1][:, 0:128], wqk[:, 0, :], ident[:, :])
                pe.transpose(bank[1][:, 128:256], wqk[:, 1, :], ident[:, :]).then_inc(w_t, 1)
                pe.wait_ge(w_tc, 2)
                pe.matmul(bank[2][:, 0:128], wqk_t[:, 0, :], wqk_t[:, 1, :], start=True, stop=True).then_inc(w_m, 1)

            @block.vector
            def _(v):
                v.memset(zero[:, :], 0.0).then_inc(zero_done, 1)
                v.memset(e_sb[:, NT - 1, :], 0.0).then_inc(e_zero, 1)
                v.wait_ge(iota_done, 2)
                v.tensor_copy(pos[:, :], pos_i[:, :]).then_inc(prep_c, 1)
                v.tensor_copy(part[:, :], part_i[:, :]).then_inc(prep_c, 1)
                v.wait_ge(rows_in, 96)
                v.tensor_copy(rows_f[:, :, :], rows_i[:, :, :, :].rearrange("r d h c -> r (d h) c")
                              ).then_inc(rows_f_done, 1)
                v.wait_ge(prep_c, 2)
                v.tensor_scalar(ident[:, :], pos[:, 0:128], part[:, 0:1], None, ALU.is_equal).then_inc(const_done, 1)
                v.tensor_scalar(spare[:, :], part[:, :], float(N), None, ALU.add).then_inc(const_done, 1)
                for a in range(Q):
                    v.tensor_scalar(before[:, a, :], pos[:, :], part[:, a:a + 1], None, ALU.is_lt
                                    ).then_inc(const_done, 1)
                for i in range(2):
                    v.memset(z[i][:, :, :], 0.0).then_inc(z_set, 1)
                    v.memset(za[i][:, :, :], 0.0).then_inc(z_set, 1)
                    v.memset(attr[i][:, :, :], 1.0).then_inc(z_set, 1)
                v.wait_ge(z_set, 6)
                for i in range(2):
                    v.memset(z[i][:, :, D + H:D + H + 1], 1.0).then_inc(z_set, 1)
                v.memset(minus_half[:, :], -0.5).then_inc(z_set, 1)
                v.wait_ge(key_t_done, 1)
                v.tensor_copy(key[:, :], bank[0][:, 0:2 * NT]).then_inc(key_done, 1)
                v.wait_ge(w_in, 128)
                v.tensor_tensor(w_src[:, 0, :], w_raw[:, 0, :], w_raw[:, 2, :], ALU.add).then_inc(w_done, 1)
                v.tensor_tensor(w_dst[:, :], w_raw[:, 1, :], w_raw[:, 2, :], ALU.subtract).then_inc(w_done, 1)
                v.wait_ge(w_t, 1)
                v.tensor_copy(wqk_t[:, 0, :], bank[1][:, 0:128]).then_inc(w_tc, 1)
                v.tensor_scalar(wqk_t[:, 1, :], bank[1][:, 128:256], wa[:, 0:1], float(D) ** -0.5,
                                ALU.mult, ALU.mult).then_inc(w_tc, 1)
                v.wait_ge(w_m, 1)
                v.tensor_copy(w_src[:, 1, :], bank[2][:, 0:128]).then_inc(w_done, 1)
                v.wait_ge(const_done, 6)
                v.wait_ge(key_done, 1)
                for d in range(2):
                    o = key_v[:, (1 - d) * NS:(2 - d) * NS, :]
                    v.scalar_tensor_tensor(meta_i[:, d * NS:(d + 1) * NS, 0:Q], o, float(N), o, ALU.is_lt, ALU.mult
                                           ).then_inc(prep_w, 1)
                v.tensor_copy(meta[:, :, KEY:W], key_v).then_inc(prep_w, 1)
                v.tensor_tensor(differ[:, :], key[:, 0:NT], key[:, NT:2 * NT], ALU.not_equal).then_inc(prep_w, 1)

                def count(s, par, k):
                    v.wait_ge(kr_in[par], k * 16 + 16)
                    for i in range(KC):
                        if not (known(s) and s * KC + i < 2):
                            v.wait_ge(counted, s * KC + (i - 1))
                        for a in range(Q):
                            c = (a + 1) * 128
                            tile = s * (KC * Q) + (i * Q + a)
                            t = v.scalar_tensor_tensor(same[(par + i) % 2][:, a, 0:c],
                                                       key_rows_sb[par][:, i * ST:i * ST + c],
                                                       key[:, bass.ds(tile, 1)], before[:, a, 0:c],
                                                       ALU.is_equal, ALU.mult,
                                                       accum_out=earlier[:, bass.ds(tile, 1)])
                        t.then_inc(counted, 1)
                    v.wait_ge(counted, s * KC + KC)
                    v.sem_inc(kr_used, 1)
                steps(v, count, NS // KC)

                v.wait_ge(kr_used, NS // KC)
                put_scatter_rows(v, 0)
                v.wait_ge(e_in_sem, 32)
                v.wait_ge(prep_w, 4)
                e_v = e_sb[:, :, :].rearrange("p (s j) h -> p s (j h)", j=Q)
                for d in range(2):
                    v.tensor_copy(meta[:, d * NS:(d + 1) * NS, EV:SC], e_v).then_inc(prep_w, 1)
                v.wait_ge(prep_w, 6)
                v.tensor_tensor(e_sb[:, :, :], e_sb[:, :, :], differ[:, :].unsqueeze(2).to_broadcast([128, NT, H]),
                                ALU.mult).then_inc(prep_w, 1)
                v.wait_ge(prep_w, 7)
                for d in range(2):
                    v.tensor_copy(meta[:, d * NS:(d + 1) * NS, W:EV], e_v).then_inc(prep_w, 1)
                v.wait_ge(prep_w, 9)
                v.wait_ge(sc_set[0], 4)
                v.sem_inc(prep_v, 1)

        early_in = [sem(f"a_early_in{i}") for i in range(2)]
        sc_in = [sem(f"a_sc_in{i}") for i in range(2)]
        row_in = [sem(f"a_row_in{i}") for i in range(2)]
        attr_in = [sem(f"a_attr_in{i}") for i in range(2)]
        x_in = [sem(f"a_x_in{i}") for i in range(2)]
        scat = [sem(f"a_scat{i}") for i in range(2)]
        (turned, turned_sb, mm_done, same_set, mask_set, neg_set, ex_set, act_set, prod_set, logit_set, att_set,
         exp_set, z_ready, r_done, r_copied) = (sem("a_" + n) for n in (
             "turned", "turned_sb", "mm_done", "same_set", "mask_set", "neg_set", "ex_set", "act_set", "prod_set",
             "logit_set", "att_set", "exp_set", "z_ready", "r_done", "r_copied"))
        half_copied, att_put = sem("a_half_copied"), sem("a_att_put")
        end_in = [sem(f"a_end_in{i}") for i in range(2)]
        end_counted, sc_out = sem("a_end_counted"), sem("a_sc_out")
        t_src, t_dst, t_attr, b_h, b_t = bank[0], bank[1], bank[2], bank[3], bank[4]
        r_bank = [bank[5], bank[6]]

        with nc.Block() as block:
            @block.sync
            def _(sp):
                sp.wait_ge(agg_zeroed, NS * 16)

                def load_sc(s, par, k):
                    if not (known(k) and k == 0):
                        sp.wait_ge(scat[par], k * 64)
                        sp.sem_inc(sp_gate, 1)
                    sp.dma_start(sc_row[par][:, :], meta_d[:, bass.ds(s, 1), SC:META]).then_inc(sc_in[par], 16)

                def load(s, par, k):
                    again = not (known(k) and k == 0)
                    if again:
                        sp.wait_ge(x_in[par], k * (8 * 16))
                        sp.sem_inc(sp_gate, 1)
                        sp.wait_ge(turned, s - 1)
                        sp.sem_inc(sp_gate, 1)
                        sp.wait_ge(same_set, s - 1)
                        sp.sem_inc(sp_gate, 1)
                        sp.wait_ge(mask_set, s - 1)
                        sp.sem_inc(sp_gate, 1)
                    sp.dma_start(src_row[par][:, :], meta_d[:, bass.ds(s + NS, 1), 0:Q].bitcast(I32)
                                 ).then_inc(early_in[par], 16)
                    sp.dma_start(early[par][:, :], meta_d[:, bass.ds(s, 1), 0:SC]).then_inc(early_in[par], 16)
                    if known(s) and s == NS - 1:
                        sp.dma_start(attr[par][:, 0:Q - 1, 0:EF],
                                     ea_in[s * ST:s * ST + (Q - 1) * 128, 0:EF]
                                     .rearrange("(j p) f -> p j f", p=128)).then_inc(attr_in[par], 16)
                        sp.dma_start(attr[par][:, Q - 1, 0:EF], ea_in[0:128, 0:EF]).then_inc(attr_in[par], 16)
                        sp.wait_ge(attr_in[par], k * 16 + 32)
                        sp.sem_inc(sp_gate, 1)
                        sp.dma_start(attr[par][0:TAIL, Q - 1, 0:EF], ea_in[E - TAIL:E, 0:EF]
                                     ).then_inc(attr_in[par], 16)
                    else:
                        sp.dma_start(attr[par][:, :, 0:EF], ea_in[bass.ds(s * ST, ST), 0:EF]
                                     .rearrange("(j p) f -> p j f", p=128)).then_inc(attr_in[par], 16)
                    sp.dma_start(key_row[par][:, :], key_rows[bass.ds(s * ST, ST)]
                                 .rearrange("(o n) -> o n", o=1).to_broadcast([128, ST])).then_inc(row_in[par], 16)
                    if again:
                        sp.wait_ge(end_counted, s - 1)
                        sp.sem_inc(sp_gate, 1)
                    sp.dma_start(key_rows_sb[par][:, 0:ST], key_rows[bass.ds(s * ST + NP, ST)]
                                 .rearrange("(o n) -> o n", o=1).to_broadcast([128, ST])).then_inc(end_in[par], 16)
                    if not (known(s) and s < 2):
                        load_sc(s - 2, par, k - 1)
                steps(sp, load, NS, peel=2)
                for s in (NS - 2, NS - 1):
                    load_sc(s, s % 2, s // 2)
                sp.wait_ge(sc_set[1], 4)
                sp.dma_start(meta_d[:, NS:2 * NS, SC:META], meta[:, NS:2 * NS, SC:META]).then_inc(sc_out, 16)
                sp.wait_ge(sc_out, 16)

            @block.gpsimd
            def _(g):
                def scatter(s, par, k):
                    g.wait_ge(sc_in[par], k * 16 + 16)
                    g.sem_inc(pool_gate, 1)
                    g.wait_ge(r_copied, s + 1)
                    g.sem_inc(pool_gate, 1)
                    if not (known(s) and s == 0):
                        g.wait_ge(scat[1 - par], (k + par) * 64)
                    g.sem_inc(pool_gate, 1)
                    for j in range(Q):
                        g.indirect_dma_start(agg[:, :], bass.IndirectOffsetOnAxis(
                            ap=sc_row[par][:, j:j + 1].bitcast(I32), axis=0),
                            summed_a[par][:, j, :], None, compute_op=ALU.add).then_inc(scat[par], 16)

                def step(s, par, k):
                    g.wait_ge(early_in[par], k * 32 + 32)
                    g.sem_inc(pool_gate, 1)
                    if not (known(k) and k == 0):
                        g.wait_ge(turned, s - 1)
                    g.sem_inc(pool_gate, 1)
                    for j in range(Q):
                        g.indirect_dma_start(xs[par][:, j, 0:D], None, x[:, :], bass.IndirectOffsetOnAxis(
                            ap=src_row[par][:, j:j + 1], axis=0)).then_inc(x_in[par], 16)
                    if not (known(s) and s < 3):
                        scatter(s - 3, 1 - par, k - 2 + par)
                    for j in range(Q):
                        g.indirect_dma_start(xd[par][:, j, :], None, x[:, :], bass.IndirectOffsetOnAxis(
                            ap=early[par][:, j:j + 1].bitcast(I32), axis=0)).then_inc(x_in[par], 16)
                steps(g, step, NS, peel=2)
                for s in (NS - 3, NS - 2, NS - 1):
                    scatter(s, s % 2, s // 2)
                for i in range(2):
                    g.wait_ge(scat[i], (NS + 1 - i) // 2 * 64)

            @block.tensor
            def _(pe):
                def add_up(s, par):
                    pe.wait_ge(same_set, s + 1)
                    if not (known(s) and s == 0):
                        pe.wait_ge(r_copied, s)
                    for b in range(Q):
                        for a in range(Q):
                            t = pe.matmul(r_bank[b // 2][:, b % 2 * AW:(b % 2 + 1) * AW],
                                          same[par][:, a, b * 128:(b + 1) * 128], za[par][:, a, :],
                                          start=(a == 0), stop=(a == Q - 1))
                    t.then_inc(r_done, 1)

                def step(s, par, k):
                    pe.wait_ge(x_in[par], k * 128 + 128)
                    if known(s) and s == NS - 1:
                        pe.wait_ge(attr_in[par], k * 16 + 48)
                    else:
                        pe.wait_ge(attr_in[par], k * 16 + 16)
                    for j in range(Q):
                        c = slice(j * 128, (j + 1) * 128)
                        pe.transpose(t_src[:, c], xs[par][:, j, 0:D], ident[:, :])
                        pe.transpose(t_dst[:, c], xd[par][:, j, :], ident[:, :])
                        t = pe.transpose(t_attr[0:EF + 1, c], attr[par][:, j, :], ident[:, :])
                    t.then_inc(turned, 1)
                    pe.wait_ge(turned_sb, s * 3 + 3)
                    if not (known(s) and s == 0):
                        pe.wait_ge(z_ready, s)
                    for j in range(Q):
                        c = slice(j * 128, (j + 1) * 128)
                        pe.matmul(b_h[:, c], xs_t[:, c], w_src[:, 0, :], start=True, stop=False)
                        pe.matmul(b_h[:, c], xd_t[:, c], w_dst[:, :], start=False, stop=False)
                        pe.matmul(b_h[:, c], attr_t[:, c], w_attr[:, :], start=False, stop=True)
                        t = pe.matmul(b_t[:, c], xs_t[:, c], w_src[:, 1, :], start=True, stop=True)
                    t.then_inc(mm_done, 1)
                    if not (known(s) and s == 0):
                        add_up(s - 1, 1 - par)
                steps(pe, step, NS)
                pe.wait_ge(z_ready, NS)
                add_up(NS - 1, (NS - 1) % 2)

            @block.scalar
            def _(act):
                def copy_sums(s, par, k):
                    act.wait_ge(r_done, s + 1)
                    if not (known(k) and k == 0):
                        act.wait_ge(scat[par], k * 64)
                    act.copy(summed_a[par][:, 0:2, :], r_bank[0][:, 0:2 * AW].rearrange("p (j w) -> p j w", j=2)
                             ).then_inc(half_copied, 1)
                    act.wait_ge(half_copied, s + 1)
                    act.copy(summed_a[par][:, 2:4, :], r_bank[1][:, 0:2 * AW].rearrange("p (j w) -> p j w", j=2)
                             ).then_inc(r_copied, 1)

                def step(s, par, k):
                    act.dma_start(zero_rows(u[0], s, 2 * ZP), zero[:, 0:ZR * UW]).then_inc(u_zeroed[0], 16)
                    act.wait_ge(turned, s + 1)
                    if not (known(s) and s == 0):
                        act.wait_ge(mm_done, s)
                    act.copy(xs_t[:, :], t_src[:, :]).then_inc(turned_sb, 1)
                    act.copy(xd_t[:, :], t_dst[:, :]).then_inc(turned_sb, 1)
                    act.copy(attr_t[:, :], t_attr[0:EF + 1, :]).then_inc(turned_sb, 1)
                    act.wait_ge(neg_set, s + 1)
                    act.activation(ex[:, :], neg[:, :], ACT.Exp).then_inc(ex_set, 1)
                    if not (known(s) and s == 0):
                        copy_sums(s - 1, 1 - par, k - 1 + par)
                    act.wait_ge(logit_set, s * Q + Q)
                    act.activation(att[:, :], logit[:, :], ACT.Tanh).then_inc(att_set, 1)
                    act.wait_ge(att_set, s + 1)
                    act.activation(exp_att[:, :], att[:, :], ACT.Exp).then_inc(exp_set, 1)
                steps(act, step, NS, peel=2)
                copy_sums(NS - 1, (NS - 1) % 2, (NS - 1) // 2)

            @block.vector
            def _(v):
                def step(s, par, k):
                    v.wait_ge(attr_in[par], k * 16 + (48 if known(s) and s == NS - 1 else 16))
                    v.tensor_scalar(mask[:, :], attr[par][:, :, 0], 8.0, None, ALU.is_lt).then_inc(mask_set, 1)
                    v.wait_ge(row_in[par], k * 16 + 16)
                    v.wait_ge(early_in[par], k * 32 + 32)
                    if not (known(k) and k == 0):
                        v.wait_ge(r_done, s - 1)
                    for a in range(Q):
                        t = v.tensor_scalar(same[par][:, a, :], key_row[par][:, :], early[par][:, KEY + a:KEY + a + 1],
                                            None, ALU.is_equal)
                    t.then_inc(same_set, 1)
                    v.wait_ge(mm_done, s + 1)
                    v.tensor_scalar(neg[:, :], b_h[:, :], 0.0, None, ALU.min).then_inc(neg_set, 1)
                    v.wait_ge(ex_set, s + 1)
                    v.scalar_tensor_tensor(act_f[:, :], b_h[:, :], 0.0, ex[:, :], ALU.max, ALU.add
                                           ).then_inc(act_set, 1)
                    v.wait_ge(act_set, s * (Q + 1) + 1)
                    v.wait_ge(mask_set, s + 1)
                    for j in range(Q):
                        c = slice(j * 128, (j + 1) * 128)
                        v.tensor_scalar(act_f[:, c], act_f[:, c], -1.0, mask[:, j:j + 1], ALU.add, ALU.mult
                                        ).then_inc(act_set, 1)
                    v.wait_ge(act_set, s * (Q + 1) + Q + 1)
                    for j in range(Q):
                        c = slice(j * 128, (j + 1) * 128)
                        v.tensor_tensor_reduce(prod[:, c], b_t[:, c], act_f[:, c], 1.0, 0.0, ALU.mult, ALU.add,
                                               logit[:, j:j + 1]).then_inc(logit_set, 1)
                    v.wait_ge(exp_set, s + 1)
                    v.tensor_copy(za[par][:, :, D], att[:, :]).then_inc(att_put, 1)
                    v.wait_ge(att_put, s + 1)
                    v.tensor_tensor(za[par][:, :, 0:D], act_f[:, :].rearrange("p (j f) -> p j f", j=Q),
                                    exp_att[:, :].unsqueeze(2).to_broadcast([128, Q, D]), ALU.mult
                                    ).then_inc(z_ready, 1)
                    v.wait_ge(end_in[par], k * 16 + 16)
                    if not (known(s) and s < 2):
                        v.wait_ge(end_counted, s - 1)
                    for a in range(Q):
                        c = (a + 1) * 128
                        t = v.scalar_tensor_tensor(
                            key_rows_sb[par][:, (a + 1) * ST:(a + 1) * ST + c].bitcast(F32),
                            key_rows_sb[par][:, 0:c], key[:, bass.ds(s * Q + (NT + a), 1)], before[:, a, 0:c],
                            ALU.is_equal, ALU.mult, accum_out=earlier[:, bass.ds(s * Q + (NT + a), 1)])
                    t.then_inc(end_counted, 1)
                steps(v, step, NS)
                v.wait_ge(end_counted, NS)
                put_scatter_rows(v, 1)

        def shape(s):
            return (NREST, 1) if known(s) and s == NCH else (128, R)

        def chunk(a, s, w):
            if known(s) and s == NCH:
                return a[NMAIN:N, 0:w].rearrange("(p r) f -> p r f", r=1)
            v = a[0:NMAIN, 0:w].rearrange("(p c r) f -> p c r f", p=128, r=R)[:, bass.ds(s, 1), :, :]
            return v.rearrange("p c r f -> p (c r) f")

        def layernorm(tag, write_to):
            stat_set, mv_set, gate, eps_set, pow_set, root_set, normed_set = (sem(tag + n) for n in (
                "stat_set", "mv_set", "v_gate", "eps_set", "pow_set", "root_set", "normed_set"))
            written = [sem(f"{tag}written{i}") for i in range(2)]

            def sums(v, s, par, res_set, res_value):
                P, RR = shape(s)
                v.wait_ge(res_set, res_value)
                for r in range(RR):
                    t = v.bn_stats(stats[0:P, r, :], res[par][0:P, r, :])
                t.then_inc(stat_set, 1)
                v.wait_ge(stat_set, s + 1)
                if not (known(s) and s < 2):
                    v.wait_ge(eps_set, s * 2 - 2)
                v.sem_inc(gate, 1)
                for r in range(RR):
                    t = v.bn_aggr(mv[par][0:P, r, :], stats[0:P, r, :])
                t.then_inc(mv_set, 1)

            def root(g, s, par):
                P, RR = shape(s)
                g.wait_ge(mv_set, s + 1)
                g.sem_inc(pool_gate, 1)
                if not (known(s) and s < 2):
                    g.wait_ge(normed_set, s - 1)
                    g.sem_inc(pool_gate, 1)
                g.tensor_scalar(rstd[par][0:P, 0:RR], mv[par][0:P, 0:RR, 1], EPS, None, ALU.add).then_inc(eps_set, 1)
                g.tensor_scalar(shift[par][0:P, 0:RR], mv[par][0:P, 0:RR, 0], -1.0, None, ALU.mult
                                ).then_inc(eps_set, 1)
                g.wait_ge(eps_set, s * 2 + 2)
                g.sem_inc(pool_gate, 1)
                g.tensor_tensor(rstd[par][0:P, 0:RR], rstd[par][0:P, 0:RR], minus_half[0:P, 0:RR], ALU.pow
                                ).then_inc(pow_set, 1)
                g.wait_ge(pow_set, s + 1)
                g.sem_inc(pool_gate, 1)
                g.tensor_tensor(shift[par][0:P, 0:RR], shift[par][0:P, 0:RR], rstd[par][0:P, 0:RR], ALU.mult
                                ).then_inc(root_set, 1)

            def scale(act, s, par, uses):
                P, RR = shape(s)
                act.wait_ge(root_set, s + 1)
                if not (known(s) and s < 2):
                    act.wait_ge(written[par], uses * 16)
                for r in range(RR):
                    t = act.activation(normed[par][0:P, r, :], res[par][0:P, r, :], ACT.Identity,
                                       bias=shift[par][0:P, r:r + 1], scale=rstd[par][0:P, r:r + 1])
                t.then_inc(normed_set, 1)

            def write(sp, s, par):
                P, RR = shape(s)
                sp.wait_ge(normed_set, s + 1)
                sp.sem_inc(sp_gate, 1)
                sp.dma_start(chunk(write_to, s, D), normed[par][0:P, 0:RR, :]).then_inc(written[par], 16)

            return sums, root, scale, write, normed_set, written

        chunk_in = [sem(f"n_chunk_in{i}") for i in range(4)]
        xa_t_half, biased = sem("n_xa_t_half"), sem("n_biased")
        decay_set, xa_set, xa_turned, xa_t_set, node_mm, res_set = (sem("n_" + n) for n in (
            "decay_set", "xa_set", "xa_turned", "xa_t_set", "node_mm", "res_set"))
        sums, root, scale, write, normed_set, written = layernorm("n_", x1)

        def uses(s, slot, k):
            return k * 2 + slot // 2

        with nc.Block() as block:
            @block.sync
            def _(sp):
                def step(s, slot, k):
                    P, RR = shape(s)
                    if not (known(k) and k == 0):
                        sp.wait_ge(res_set, s - 3)
                        sp.sem_inc(sp_gate, 1)
                    sp.dma_start(xc[slot][0:P, 0:RR, :], chunk(x, s, D)).then_inc(chunk_in[slot], 16)
                    sp.dma_start(agc[slot][0:P, 0:RR, :], chunk(agg, s, AW)).then_inc(chunk_in[slot], 16)
                    if not (known(s) and s < 4):
                        write(sp, s - 4, slot % 2)
                steps(sp, step, NCH + 1, 4)
                for s in range(NCH - 3, NCH + 1):
                    write(sp, s, s % 2)
                for i in range(2):
                    sp.wait_ge(written[i], (NCH + 2 - i) // 2 * 16)

            @block.gpsimd
            def _(g):
                def step(s, slot, k):
                    P, RR = shape(s)
                    if not (known(s) and s < 2):
                        root(g, s - 2, slot % 2)
                    g.wait_ge(xa_set, s + 1)
                    g.sem_inc(pool_gate, 1)
                    g.tensor_tensor(xc[slot][0:P, 0:RR, :], xc[slot][0:P, 0:RR, :],
                                    bu_all[0:P, :].unsqueeze(1).to_broadcast([P, RR, D]), ALU.add
                                    ).then_inc(biased, 1)
                steps(g, step, NCH + 1, 4)
                for s in (NCH - 1, NCH):
                    root(g, s, s % 2)

            @block.scalar
            def _(act):
                def step(s, slot, k):
                    P, RR = shape(s)
                    act.wait_ge(chunk_in[slot], k * 32 + 32)
                    act.activation(decay[0:P, slot, 0:RR], agc[slot][0:P, 0:RR, D], ACT.Exp, scale=-1.0
                                   ).then_inc(decay_set, 1)
                    if not (known(s) and s < 3):
                        sl, kk = back(slot, k, 3, 4)
                        scale(act, s - 3, sl % 2, uses(s - 3, sl, kk))
                    act.wait_ge(xa_turned, s + 1)
                    if not (known(s) and s == 0):
                        act.wait_ge(node_mm, s)
                    b = 4 * (slot % 2)
                    for h in range(-(-RR // 4)):
                        c = min(RR - 4 * h, 4) * 128
                        t = act.copy(xa_t[:, h * 512:h * 512 + c], bank[b + h][:, 0:c])
                        t.then_inc(xa_t_half, 1)
                    act.wait_ge(xa_t_half, s * 2 + 2 if not (known(s) and s == NCH) else s * 2 + 1)
                    act.sem_inc(xa_t_set, 1)
                steps(act, step, NCH + 1, 4)
                for s in range(NCH - 2, NCH + 1):
                    scale(act, s, s % 2, s // 2)

            @block.tensor
            def _(pe):
                def step(s, slot, k):
                    P, RR = shape(s)
                    b = 4 * (slot % 2)
                    pe.wait_ge(xa_set, s + 1)
                    for r in range(RR):
                        t = pe.transpose(bank[b + r // 4][:, r % 4 * 128:r % 4 * 128 + P], xa[0:P, r, :],
                                         ident[0:P, 0:P])
                    t.then_inc(xa_turned, 1)
                    pe.wait_ge(xa_t_set, s + 1)
                    if not (known(s) and s < 2):
                        pe.wait_ge(res_set, s - 1)
                    for r in range(RR):
                        o = bank[b + 2 + r // 4][0:P, r % 4 * 128:r % 4 * 128 + 128]
                        t = pe.matmul(o, xa_t[:, r * 128:r * 128 + P], wu[:, :], start=True, stop=True)
                    t.then_inc(node_mm, 1)
                steps(pe, step, NCH + 1, 4)

            @block.vector
            def _(v):
                def make_xa(s, slot, k):
                    P, RR = shape(s)
                    v.wait_ge(decay_set, s + 1)
                    if not (known(s) and s == 0):
                        v.wait_ge(xa_turned, s)
                    for r in range(RR):
                        t = v.scalar_tensor_tensor(xa[0:P, r, :], agc[slot][0:P, r, 0:D],
                                                   decay[0:P, slot, r:r + 1], xc[slot][0:P, r, :],
                                                   ALU.mult, ALU.add)
                    t.then_inc(xa_set, 1)

                def make_res(s, slot, k):
                    P, RR = shape(s)
                    b = 4 * (slot % 2)
                    v.wait_ge(node_mm, s + 1)
                    v.wait_ge(biased, s + 1)
                    if not (known(s) and s < 2):
                        v.wait_ge(normed_set, s - 1)
                    for h in range(-(-RR // 4)):
                        c = min(RR - 4 * h, 4)
                        t = v.tensor_tensor(res[slot % 2][0:P, 4 * h:4 * h + c, :], xc[slot][0:P, 4 * h:4 * h + c, :],
                                            bank[b + 2 + h][0:P, 0:c * 128].rearrange("p (r f) -> p r f", f=128),
                                            ALU.add)
                    t.then_inc(res_set, 1)
                    sums(v, s, slot % 2, res_set, s + 1)

                def step(s, slot, k):
                    make_xa(s, slot, k)
                    if not (known(s) and s < 1):
                        make_res(s - 1, *back(slot, k, 1, 4))
                steps(v, step, NCH + 1, 4)
                make_res(NCH, NCH % 4, NCH // 4)

        NH = 2 * NS
        early_in = [sem(f"h_early_in{i}") for i in range(2)]
        sc_in = [sem(f"h_sc_in{i}") for i in range(2)]
        row_in = [sem(f"h_row_in{i}") for i in range(2)]
        v_in = [sem(f"h_v_in{i}") for i in range(2)]
        scat = [sem(f"h_scat{i}") for i in range(2)]
        same_set, e_put, inv_set, wn_set, z_ready, r_done, half_copied, r_copied, z_cleared = (sem("h_" + n) for n in (
            "same_set", "e_put", "inv_set", "wn_set", "z_ready", "r_done", "half_copied", "r_copied", "z_cleared"))

        def hop(h):
            source = x1 if h == 0 else u[h - 1]
            width = D if h == 0 else UW
            target = u[h] if h < 3 else u[1]
            share = 1.0 if h < 3 else 1.0 / 12
            base, kb = h * NH, h * (NH // 2)

            with nc.Block() as block:
                @block.sync
                def _(sp):
                    def load_sc(s, par, k):
                        if not (known(k) and k == 0):
                            sp.wait_ge(scat[par], (k + kb) * 64)
                            sp.sem_inc(sp_gate, 1)
                        sp.dma_start(sc_row[par][:, :], meta_d[:, bass.ds(s, 1), SC:META]).then_inc(sc_in[par], 16)

                    def load(s, par, k):
                        again = not (known(k) and k == 0)
                        if again:
                            sp.wait_ge(v_in[par], (k + kb) * 64)
                            sp.sem_inc(sp_gate, 1)
                            sp.wait_ge(same_set, s - 1 + base)
                            sp.sem_inc(sp_gate, 1)
                            sp.wait_ge(z_ready, s - 1 + base)
                            sp.sem_inc(sp_gate, 1)
                            if h < 3:
                                sp.wait_ge(e_put, s - 1 + base)
                            sp.sem_inc(sp_gate, 1)
                        sp.dma_start(early[par][:, :], meta_d[:, bass.ds(s, 1), 0:SC]).then_inc(early_in[par], 16)
                        sp.dma_start(key_row[par][:, :], key_rows[bass.ds(s * ST, ST)]
                                     .rearrange("(o n) -> o n", o=1).to_broadcast([128, ST])).then_inc(row_in[par], 16)
                        if not (known(s) and s < 1):
                            load_sc(s - 1, *back(par, k, 1, 2))
                    steps(sp, load, NH, peel=2)
                    load_sc(NH - 1, 1, NH // 2 - 1)

                @block.gpsimd
                def _(g):
                    if h < 3:
                        g.wait_ge(u_zeroed[h], (NS if h == 0 else NH) * 16)

                    def scatter(s, par, k):
                        g.wait_ge(sc_in[par], (k + kb) * 16 + 16)
                        g.sem_inc(pool_gate, 1)
                        g.wait_ge(r_copied, s + 1 + base)
                        g.sem_inc(pool_gate, 1)
                        if not (known(s) and s == 0):
                            g.wait_ge(scat[1 - par], (k + kb + par) * 64)
                        g.sem_inc(pool_gate, 1)
                        for j in range(Q):
                            g.indirect_dma_start(target[:, :], bass.IndirectOffsetOnAxis(
                                ap=sc_row[par][:, j:j + 1].bitcast(I32), axis=0),
                                summed[par][:, j, :], None, compute_op=ALU.add).then_inc(scat[par], 16)

                    def step(s, par, k):
                        g.wait_ge(early_in[par], (k + kb) * 16 + 16)
                        g.sem_inc(pool_gate, 1)
                        if not (known(k) and k == 0):
                            g.wait_ge(z_ready, s - 1 + base)
                        g.sem_inc(pool_gate, 1)
                        for j in range(Q):
                            g.indirect_dma_start(xs[par][:, j, 0:width], None, source[:, :],
                                                 bass.IndirectOffsetOnAxis(
                                ap=early[par][:, j:j + 1].bitcast(I32), axis=0)).then_inc(v_in[par], 16)
                        if not (known(s) and s < 2):
                            scatter(s - 2, par, k - 1)
                    steps(g, step, NH, peel=2)
                    for s in (NH - 2, NH - 1):
                        scatter(s, s % 2, s // 2)
                    for i in range(2):
                        g.wait_ge(scat[i], (h + 1) * (NH // 2) * 64)

                @block.tensor
                def _(pe):
                    def step(s, par, k):
                        pe.wait_ge(same_set, s + 1 + base)
                        pe.wait_ge(z_ready, s + 1 + base)
                        if h < 3:
                            pe.wait_ge(e_put, s + 1 + base)
                        if not (known(s) and s < 2):
                            pe.wait_ge(r_copied, s - 1 + base)
                        for b in range(Q):
                            for a in range(Q):
                                t = pe.matmul(bank[2 * par + b // 2][:, b % 2 * UW:(b % 2 + 1) * UW],
                                              same[par][:, a, b * 128:(b + 1) * 128], z[par][:, a, :],
                                              start=(a == 0), stop=(a == Q - 1))
                        t.then_inc(r_done, 1)
                    steps(pe, step, NH)

                @block.scalar
                def _(act):
                    def copy_sums(s, par, k):
                        act.wait_ge(r_done, s + 1 + base)
                        if not (known(k) and k == 0):
                            act.wait_ge(scat[par], (k + kb) * 64)
                        for i in range(2):
                            act.copy(summed[par][:, 2 * i:2 * i + 2, :],
                                     bank[2 * par + i][:, 0:2 * UW].rearrange("p (j w) -> p j w", j=2)
                                     ).then_inc(half_copied, 1)
                        act.wait_ge(half_copied, s * 2 + 2 + 2 * base)
                        act.sem_inc(r_copied, 1)

                    def step(s, par, k):
                        if h < 2:
                            act.dma_start(zero_rows(u[h + 1], s, ZP), zero[0:ZP, 0:ZR * UW]).then_inc(u_zeroed[h + 1], 16)
                        if h < 3:
                            act.wait_ge(early_in[par], (k + kb) * 16 + 16)
                            if not (known(s) and s < 2):
                                act.wait_ge(r_done, s - 1 + base)
                            act.copy(z[par][:, :, D:D + H],
                                     early[par][:, EV:SC].rearrange("p (j h) -> p j h", j=Q)).then_inc(e_put, 1)
                        if not (known(s) and s < 1):
                            copy_sums(s - 1, *back(par, k, 1, 2))
                    steps(act, step, NH)
                    copy_sums(NH - 1, 1, NH // 2 - 1)

                @block.vector
                def _(v):
                    if h == 3:
                        for i in range(2):
                            v.memset(z[i][:, :, D:D + H + 1], 0.0).then_inc(z_cleared, 1)
                        v.wait_ge(z_cleared, 2)

                    def step(s, par, k):
                        v.wait_ge(row_in[par], (k + kb) * 16 + 16)
                        v.wait_ge(early_in[par], (k + kb) * 16 + 16)
                        if not (known(s) and s < 2):
                            v.wait_ge(r_done, s - 1 + base)
                        for a in range(Q):
                            t = v.tensor_scalar(same[par][:, a, :], key_row[par][:, :],
                                                early[par][:, KEY + a:KEY + a + 1], None, ALU.is_equal)
                        t.then_inc(same_set, 1)
                        v.wait_ge(v_in[par], (k + kb) * 64 + 64)
                        weight = early[par][:, W:EV].rearrange("p (j h) -> p j h", j=Q)
                        if h > 0:
                            sum_e = xs[par][:, :, D:D + H]
                            v.scalar_tensor_tensor(inv[:, :, :], sum_e, 0.0, sum_e, ALU.is_equal, ALU.add
                                                   ).then_inc(inv_set, 1)
                            v.wait_ge(inv_set, (s + base - NH) * 2 + 1)
                            v.reciprocal(inv[:, :, :], inv[:, :, :]).then_inc(inv_set, 1)
                            v.wait_ge(inv_set, (s + base - NH) * 2 + 2)
                            v.scalar_tensor_tensor(wn[:, :, :], weight, share, inv[:, :, :], ALU.mult, ALU.mult
                                                   ).then_inc(wn_set, 1)
                            v.wait_ge(wn_set, s + 1 + base - NH)
                            weight = wn[:, :, :]
                        for j in range(Q):
                            t = v.tensor_tensor(z[par][:, j, 0:D].rearrange("p (h f) -> p h f", h=H),
                                                xs[par][:, j, 0:D].rearrange("p (h f) -> p h f", h=H),
                                                weight[:, j, :].unsqueeze(2).to_broadcast([128, H, HF]), ALU.mult)
                        t.then_inc(z_ready, 1)
                    steps(v, step, NH)

        for h in range(4):
            hop(h)

        chunk_in = [sem(f"o_chunk_in{i}") for i in range(4)]
        b_set, res_set = sem("o_b_set"), sem("o_res_set")
        sums, root, scale, write, normed_set, written = layernorm("o_", out)

        with nc.Block() as block:
            @block.sync
            def _(sp):
                def step(s, slot, k):
                    P, RR = shape(s)
                    if not (known(k) and k == 0):
                        sp.wait_ge(res_set, s - 3)
                        sp.sem_inc(sp_gate, 1)
                    sp.dma_start(xc[slot][0:P, 0:RR, :], chunk(x1, s, D)).then_inc(chunk_in[slot], 16)
                    for i in range(3):
                        sp.dma_start(uc[i][slot][0:P, 0:RR, :], chunk(u[i], s, UW)).then_inc(chunk_in[slot], 16)
                    if not (known(s) and s < 4):
                        write(sp, s - 4, slot % 2)
                steps(sp, step, NCH + 1, 4)
                for s in range(NCH - 3, NCH + 1):
                    write(sp, s, s % 2)
                for i in range(2):
                    sp.wait_ge(written[i], (NCH + 2 - i) // 2 * 16)

            @block.gpsimd
            def _(g):
                steps(g, lambda s, slot, k: root(g, s, slot % 2), NCH + 1, 4)

            @block.scalar
            def _(act):
                steps(act, lambda s, slot, k: scale(act, s, slot % 2, uses(s, slot, k)), NCH + 1, 4)

            @block.vector
            def _(v):
                B = 7

                def make_res(s, slot, k):
                    P, RR = shape(s)
                    u0, u1, u2 = (uc[i][slot][0:P, 0:RR, :] for i in range(3))
                    iso, ci = isolated[0:P, 0:RR], cinv[0:P, 0:RR, :]
                    v.wait_ge(chunk_in[slot], k * 64 + 64)
                    v.tensor_scalar(iso, u0[:, :, D + H], 0.0, None, ALU.is_equal).then_inc(b_set, 1)
                    v.wait_ge(b_set, s * B + 1)
                    v.tensor_tensor(ci, u0[:, :, D:D + H], iso.unsqueeze(2).to_broadcast([P, RR, H]), ALU.add
                                    ).then_inc(b_set, 1)
                    v.scalar_tensor_tensor(u0[:, :, 0:D], u1[:, :, 0:D], 0.5, u0[:, :, 0:D], ALU.mult, ALU.add
                                           ).then_inc(b_set, 1)
                    v.wait_ge(b_set, s * B + 3)
                    v.reciprocal(ci, ci).then_inc(b_set, 1)
                    v.scalar_tensor_tensor(u0[:, :, 0:D], u2[:, :, 0:D], 1.0 / 6, u0[:, :, 0:D], ALU.mult, ALU.add
                                           ).then_inc(b_set, 1)
                    v.wait_ge(b_set, s * B + 5)
                    for r in range(RR):
                        t = v.tensor_tensor(u0[:, r, 0:D].rearrange("p (h f) -> p h f", h=H),
                                            u0[:, r, 0:D].rearrange("p (h f) -> p h f", h=H),
                                            ci[:, r, :].unsqueeze(2).to_broadcast([P, H, HF]), ALU.mult)
                    t.then_inc(b_set, 1)
                    v.wait_ge(b_set, s * B + 6)
                    if not (known(s) and s < 2):
                        v.wait_ge(normed_set, s - 1)
                    v.scalar_tensor_tensor(res[slot % 2][0:P, 0:RR, :], xc[slot][0:P, 0:RR, :], 2.0, u0[:, :, 0:D],
                                           ALU.mult, ALU.add).then_inc(res_set, 1)
                    v.sem_inc(b_set, 1)
                    sums(v, s, slot % 2, res_set, s + 1)

                steps(v, make_res, NCH + 1, 4)


_INS = ['x', 'src', 'dst', 'edge_attr3_4x1', 'edge_attr_70', 'L0_gnn_Wf', 'L0_gnn_bf', 'L0_gnn_Wq', 'L0_gnn_Wk',
        'L0_gnn_Wa', 'L0_gnn_Wu', 'L0_gnn_bu']


def kernel(**inputs):
    import numpy as _np
    import concourse.bacc as _bacc
    from concourse import mybir as _mybir
    from concourse.bass_utils import run_bass_kernel_spmd as _run

    nc = _bacc.Bacc("TRN2", target_bir_lowering=False, num_devices=1)
    arrays, args = {}, []
    for name in _INS:
        a = _np.ascontiguousarray(inputs[name])
        arrays[f"in_{name}_dram"] = a
        args.append(nc.dram_tensor(f"in_{name}_dram", a.shape, _mybir.dt.from_np(a.dtype), kind="ExternalInput").ap())
    args.append(nc.dram_tensor("out_0_dram", (N, D), _mybir.dt.float32, kind="ExternalOutput").ap())
    build(nc, *args)
    r = _run(nc, [arrays], core_ids=[0])
    return r.results[0]["out_0_dram"]
```
